# Optimizing a Trainium2 kernel written in Bass

```python
import numpy as np
import jax
import jax.numpy as jnp

def _softmax(x, axis=-1):
    return jax.nn.softmax(x, axis=axis)

def _gelu(x):
    return jax.nn.gelu(x, approximate=True)

def _silu(x):
    return jax.nn.silu(x)

def _sigmoid(x):
    return jax.nn.sigmoid(x)

def _layernorm(x, axis=-1, eps=1e-05):
    m = jnp.mean(x, axis=axis, keepdims=True)
    v = jnp.var(x, axis=axis, keepdims=True)
    return (x - m) / jnp.sqrt(v + eps)

def _scatter_add(tgt, idx, src, axis=0):
    return tgt.at[idx].add(src)

def _segment_sum(src, seg, n):
    return jax.ops.segment_sum(src, seg, n)
kernel_name = 'mk_flamingo_gated_d2_seqx_r4_20f384'

def setup_inputs(seed: int=0):
    np.random.seed(seed)
    _w = jnp.asarray

    def _rec_inputs():
        import jax
        import jax.numpy as jnp
        _rk = jax.random.key(seed)
        x = 4.136e-05 + 0.9999 * jax.random.normal(jax.random.fold_in(_rk, 1), (16, 256, 256), jnp.float32)
        _lenS = 256 - jax.random.randint(jax.random.fold_in(_rk, 7), (16,), 0, max(1, 256 // 4) + 1, jnp.int32)
        _lenS2 = 256 - jax.random.randint(jax.random.fold_in(_rk, 8), (16,), 0, max(1, 256 // 4) + 1, jnp.int32)
        _ctx_2048P = jax.random.normal(jax.random.fold_in(_rk, 11), (16, 16, 512), jnp.float32)
        _ctx_2048c = jax.random.dirichlet(jax.random.fold_in(_rk, 511), 0.3 * jnp.ones((16,), jnp.float32), (16, 256))
        _ctx_2048t = jnp.einsum('bsk,bkd->bsd', _ctx_2048c, _ctx_2048P)
        _ctx_2048t = _ctx_2048t * jax.lax.rsqrt(jnp.mean(jnp.square(_ctx_2048t)) + 1e-12) * 0.953939
        ctx_2048 = -0.000392918 + 0.999932 * (_ctx_2048t + 0.3 * jax.random.normal(jax.random.fold_in(_rk, 611), (16, 256, 512), jnp.float32))
        itok_Bx1_68_817 = jax.random.randint(jax.random.fold_in(_rk, 12), (16, 1), 68, 818, jnp.int32)
        _g = jax.random.normal(jax.random.fold_in(_rk, 9001), (2, 2), jnp.float32)
        _g = jnp.sign(_g) * jnp.maximum(jnp.abs(_g), 1.0) + (_g == 0) * 1.0
        g_xattn = _g[0]
        g_ffn = _g[1]
        return (x, ctx_2048, itok_Bx1_68_817, g_xattn, g_ffn)
    x, ctx_2048, itok_Bx1_68_817, g_xattn, g_ffn = _rec_inputs()

    def _L0_xattn_setup():
        import jax, jax.numpy as jnp
        import numpy as np
        UNITS = 256
        NUM_HEADS = 16
        MASK_VALUE = -1000000000000.0

        def _split_heads(x, n):
            B, S, D = x.shape
            return x.reshape(B, S, n, D // n).transpose(0, 2, 1, 3)
        key = jax.random.key(seed)
        k1, k2, k3, k4 = jax.random.split(key, 4)
        B, S = (8, 256)
        memory = jax.random.normal(k1, (B, S, 2 * UNITS), dtype=jnp.float32)
        query = jax.random.normal(k2, (B, S, UNITS), dtype=jnp.float32)
        b = jax.random.normal(k3, (S,), dtype=jnp.float32)
        seq_len = jax.random.randint(k4, (B, 1), 0, S, dtype=jnp.int32)
        return {'memory': memory, 'query': query, 'b': b, 'seq_len': seq_len}
    _L0_xattn_all = _L0_xattn_setup()
    _L0_xattn_in = {k: v for k, v in _L0_xattn_all.items() if k in ('b',)}
    del _L0_xattn_all

    def _L0_ffn_setup():
        import jax, jax.numpy as jnp
        import numpy as np
        NUM_HEADS = 16
        TOP_K = 2
        key = jax.random.key(seed)
        ks = jax.random.split(key, 5)
        B, S, D, E = (4, 512, 256, 8)
        scale = 0.02
        return {'x': jax.random.normal(ks[0], (B, S, D), dtype=jnp.float32), 'W_qkv': jax.random.normal(ks[1], (D, 3 * D), dtype=jnp.float32) * scale, 'b_qkv': jnp.zeros((3 * D,), dtype=jnp.float32), 'W_gate': jax.random.normal(ks[2], (D, E), dtype=jnp.float32) * scale, 'b_gate': jnp.zeros((E,), dtype=jnp.float32), 'W_experts': jax.random.normal(ks[3], (E, D, D), dtype=jnp.float32) * scale, 'b_experts': jnp.zeros((E, D), dtype=jnp.float32)}
    _L0_ffn_all = _L0_ffn_setup()
    _L0_ffn_in = {k: v for k, v in _L0_ffn_all.items() if k in ('W_qkv', 'b_qkv', 'W_gate', 'b_gate', 'W_experts', 'b_experts')}
    del _L0_ffn_all

    def _L1_xattn_setup():
        import jax, jax.numpy as jnp
        import numpy as np
        NUM_HEADS = 16
        key = jax.random.key(seed)
        ks = jax.random.split(key, 5)
        dim = 256
        B, N, N_c = (4, 256, 64)
        x = jax.random.normal(ks[0], (B, N, dim), dtype=jnp.float32)
        context = jax.random.normal(ks[1], (B, N_c, 2 * dim), dtype=jnp.float32)
        w_qkv = jax.random.normal(ks[2], (3 * dim, dim), dtype=jnp.float32) * 0.02
        w_proj = jax.random.normal(ks[3], (dim, dim), dtype=jnp.float32) * 0.02
        b_proj = jax.random.normal(ks[4], (dim,), dtype=jnp.float32) * 0.02
        return {'x': x, 'context': context, 'w_qkv': w_qkv, 'w_proj': w_proj, 'b_proj': b_proj}
    _L1_xattn_all = _L1_xattn_setup()
    _L1_xattn_in = {k: v for k, v in _L1_xattn_all.items() if k in ('w_qkv', 'w_proj', 'b_proj')}
    del _L1_xattn_all

    def _L1_ffn_setup():
        import jax, jax.numpy as jnp
        import numpy as np
        B, S, D, H, E, K, F = (1, 256, 256, 16, 8, 2, 1024)

        def layernorm(x, g, b, eps=1e-05):
            m = x.mean(-1, keepdims=True)
            v = ((x - m) ** 2).mean(-1, keepdims=True)
            return (x - m) * jax.lax.rsqrt(v + eps) * g + b
        key = jax.random.key(seed)
        ks = jax.random.split(key, 8)
        n = lambda k, shape, sc: jax.random.normal(k, shape, dtype=jnp.float32) * sc
        return {'x': n(ks[0], (B, S, D), 1.0), 'w_qkv': n(ks[1], (D, 3 * D), D ** (-0.5)), 'w_o': n(ks[2], (D, D), D ** (-0.5)), 'g1': jnp.ones((D,), jnp.float32), 'b1': jnp.zeros((D,), jnp.float32), 'wg': n(ks[3], (D, E), D ** (-0.5)), 'w1': n(ks[4], (E, D, F), D ** (-0.5)), 'bb1': jnp.zeros((E, F), jnp.float32), 'w2': n(ks[5], (E, F, D), F ** (-0.5)), 'bb2': jnp.zeros((E, D), jnp.float32), 'g2': jnp.ones((D,), jnp.float32), 'b2': jnp.zeros((D,), jnp.float32)}
    _L1_ffn_all = _L1_ffn_setup()
    _L1_ffn_in = {k: v for k, v in _L1_ffn_all.items() if k in ('w_qkv', 'w_o', 'g1', 'b1', 'wg', 'w1', 'bb1', 'w2', 'bb2', 'g2', 'b2')}
    del _L1_ffn_all
    return {'x': x, 'ctx_2048': ctx_2048, 'itok_Bx1_68_817': itok_Bx1_68_817, 'g_xattn': g_xattn, 'g_ffn': g_ffn, 'L0_xattn_b': _L0_xattn_in['b'], 'L0_ffn_W_qkv': _L0_ffn_in['W_qkv'], 'L0_ffn_b_qkv': _L0_ffn_in['b_qkv'], 'L0_ffn_W_gate': _L0_ffn_in['W_gate'], 'L0_ffn_b_gate': _L0_ffn_in['b_gate'], 'L0_ffn_W_experts': _L0_ffn_in['W_experts'], 'L0_ffn_b_experts': _L0_ffn_in['b_experts'], 'L1_xattn_w_qkv': _L1_xattn_in['w_qkv'], 'L1_xattn_w_proj': _L1_xattn_in['w_proj'], 'L1_xattn_b_proj': _L1_xattn_in['b_proj'], 'L1_ffn_w_qkv': _L1_ffn_in['w_qkv'], 'L1_ffn_w_o': _L1_ffn_in['w_o'], 'L1_ffn_g1': _L1_ffn_in['g1'], 'L1_ffn_b1': _L1_ffn_in['b1'], 'L1_ffn_wg': _L1_ffn_in['wg'], 'L1_ffn_w1': _L1_ffn_in['w1'], 'L1_ffn_bb1': _L1_ffn_in['bb1'], 'L1_ffn_w2': _L1_ffn_in['w2'], 'L1_ffn_bb2': _L1_ffn_in['bb2'], 'L1_ffn_g2': _L1_ffn_in['g2'], 'L1_ffn_b2': _L1_ffn_in['b2']}

def reference(x, ctx_2048, itok_Bx1_68_817, g_xattn, g_ffn, L0_xattn_b, L0_ffn_W_qkv, L0_ffn_b_qkv, L0_ffn_W_gate, L0_ffn_b_gate, L0_ffn_W_experts, L0_ffn_b_experts, L1_xattn_w_qkv, L1_xattn_w_proj, L1_xattn_b_proj, L1_ffn_w_qkv, L1_ffn_w_o, L1_ffn_g1, L1_ffn_b1, L1_ffn_wg, L1_ffn_w1, L1_ffn_bb1, L1_ffn_w2, L1_ffn_bb2, L1_ffn_g2, L1_ffn_b2):
    import jax
    import jax.numpy as jnp

    def _L0_xattn_ref(memory, query, b, seq_len):
        import jax, jax.numpy as jnp
        import numpy as np
        UNITS = 256
        NUM_HEADS = 16
        MASK_VALUE = -1000000000000.0

        def _split_heads(x, n):
            B, S, D = x.shape
            return x.reshape(B, S, n, D // n).transpose(0, 2, 1, 3)
        B, S, _ = query.shape
        dh = UNITS // NUM_HEADS
        k_mem, v_mem = jnp.split(memory, 2, axis=2)
        Q = _split_heads(query, NUM_HEADS) * dh ** (-0.5)
        Kh = _split_heads(k_mem, NUM_HEADS)
        Vh = _split_heads(v_mem, NUM_HEADS)
        logits = jnp.einsum('bhqd,bhkd->bhqk', Q, Kh) + b
        valid = (jnp.arange(S)[None, :] < seq_len[:, 0:1]).astype(jnp.float32)
        logits = logits + MASK_VALUE * (1.0 - valid)[:, None, None, :]
        weights = jax.nn.softmax(logits, axis=-1)
        out = jnp.einsum('bhqk,bhkd->bhqd', weights, Vh)
        return out.transpose(0, 2, 1, 3).reshape(B, S, UNITS)

    def _L0_ffn_ref(x, W_qkv, b_qkv, W_gate, b_gate, W_experts, b_experts):
        import jax, jax.numpy as jnp
        import numpy as np
        NUM_HEADS = 16
        TOP_K = 2
        B, S, D = x.shape
        H = NUM_HEADS
        hd = D // H
        E = W_gate.shape[-1]
        qkv = (x @ W_qkv + b_qkv).reshape(B, S, 3, H, hd)
        q, k, v = (qkv[:, :, 0], qkv[:, :, 1], qkv[:, :, 2])
        attn = jnp.einsum('bqhd,bkhd->bhqk', q, k) / jnp.sqrt(jnp.asarray(hd, x.dtype))
        attn = jax.nn.softmax(attn, axis=-1)
        attn_out = jnp.einsum('bhqk,bkhd->bqhd', attn, v).reshape(B, S, D)
        gate = jax.nn.softmax(x @ W_gate + b_gate, axis=-1)
        top_g, top_i = jax.lax.top_k(gate, TOP_K)
        combine = jnp.sum(jax.nn.one_hot(top_i, E, dtype=x.dtype) * top_g[..., None], axis=2)
        expert_out = jnp.einsum('bsd,edf->bsef', x, W_experts) + b_experts
        moe_out = jnp.einsum('bsef,bse->bsf', expert_out, combine)
        return attn_out + moe_out

    def _L1_xattn_ref(x, context, w_qkv, w_proj, b_proj):
        import jax, jax.numpy as jnp
        import numpy as np
        NUM_HEADS = 16
        B, N, C = x.shape
        H = NUM_HEADS
        D = C // H
        scale = D ** (-0.5)
        qkv = (x @ w_qkv.T).reshape(B, N, 3, H, D).transpose(2, 0, 3, 1, 4)
        q, k, v = (qkv[0], qkv[1], qkv[2])
        N_c = context.shape[1]
        kv = context.reshape(B, N_c, 2, H, D).transpose(2, 0, 3, 1, 4)
        extra_k, extra_v = (kv[0], kv[1])
        k = jnp.concatenate([extra_k, k], axis=2)
        v = jnp.concatenate([extra_v, v], axis=2)
        dtype = q.dtype
        attn = jnp.einsum('bhnd,bhmd->bhnm', q * scale, k).astype(jnp.float32)
        attn = jax.nn.softmax(attn, axis=-1).astype(dtype)
        out = jnp.einsum('bhnm,bhmd->bhnd', attn, v)
        out = out.transpose(0, 2, 1, 3).reshape(B, N, C)
        return out @ w_proj.T + b_proj

    def _L1_ffn_ref(x, w_qkv, w_o, g1, b1, wg, w1, bb1, w2, bb2, g2, b2):
        import jax, jax.numpy as jnp
        import numpy as np
        B, S, D, H, E, K, F = (1, 256, 256, 16, 8, 2, 1024)

        def layernorm(x, g, b, eps=1e-05):
            m = x.mean(-1, keepdims=True)
            v = ((x - m) ** 2).mean(-1, keepdims=True)
            return (x - m) * jax.lax.rsqrt(v + eps) * g + b
        b, s, d = x.shape
        hd = d // H
        qkv = x @ w_qkv
        q, k, v = jnp.split(qkv, 3, axis=-1)
        to_heads = lambda t: t.reshape(b, s, H, hd).transpose(0, 2, 1, 3)
        q, k, v = (to_heads(q), to_heads(k), to_heads(v))
        scores = jnp.einsum('bhqd,bhkd->bhqk', q, k) / jnp.sqrt(jnp.float32(hd))
        causal = jnp.tril(jnp.ones((s, s), bool))
        scores = jnp.where(causal, scores, jnp.finfo(scores.dtype).min)
        attn = jax.nn.softmax(scores, axis=-1)
        o = jnp.einsum('bhqk,bhkd->bhqd', attn, v)
        o = o.transpose(0, 2, 1, 3).reshape(b, s, d) @ w_o
        h = layernorm(x + o, g1, b1)
        probs = jax.nn.softmax(h @ wg, axis=-1)
        topv, topi = jax.lax.top_k(probs, K)
        topv = topv / topv.sum(-1, keepdims=True)
        w = (topv[..., None] * jax.nn.one_hot(topi, E, dtype=h.dtype)).sum(-2)
        h1 = jax.nn.gelu(jnp.einsum('bsd,edf->ebsf', h, w1) + bb1[:, None, None, :])
        y = jnp.einsum('ebsf,efd->ebsd', h1, w2) + bb2[:, None, None, :]
        moe = jnp.einsum('ebsd,bse->bsd', y, w)
        return layernorm(h + moe, g2, b2)
    x = x + jnp.tanh(g_xattn[0]) * _L0_xattn_ref(ctx_2048, _layernorm(x, axis=-1), L0_xattn_b, itok_Bx1_68_817)
    x = x + jnp.tanh(g_ffn[0]) * _L0_ffn_ref(_layernorm(x, axis=-1), L0_ffn_W_qkv, L0_ffn_b_qkv, L0_ffn_W_gate, L0_ffn_b_gate, L0_ffn_W_experts, L0_ffn_b_experts)
    x = x + jnp.tanh(g_xattn[1]) * _L1_xattn_ref(_layernorm(x, axis=-1), ctx_2048, L1_xattn_w_qkv, L1_xattn_w_proj, L1_xattn_b_proj)
    x = x + jnp.tanh(g_ffn[1]) * _L1_ffn_ref(_layernorm(x, axis=-1), L1_ffn_w_qkv, L1_ffn_w_o, L1_ffn_g1, L1_ffn_b1, L1_ffn_wg, L1_ffn_w1, L1_ffn_bb1, L1_ffn_w2, L1_ffn_bb2, L1_ffn_g2, L1_ffn_b2)
    return x

_drawn_inputs = setup_inputs


def setup_inputs(seed=0):
    import zlib

    import numpy as np

    out = dict(_drawn_inputs(seed))
    spreads = {'g_ffn': (-1.0, 0.2),
     'L0_ffn_b_qkv': (0.0, 0.1),
     'L0_ffn_b_gate': (0.0, 0.1),
     'L0_ffn_b_experts': (0.0, 0.1),
     'L1_ffn_g1': (1.0, 0.2),
     'L1_ffn_b1': (0.0, 0.1),
     'L1_ffn_bb1': (0.0, 0.1),
     'L1_ffn_bb2': (0.0, 0.1),
     'L1_ffn_g2': (1.0, 0.2),
     'L1_ffn_b2': (0.0, 0.1)}
    factors = {}
    for name, (base, spread) in spreads.items():
        noise = np.random.default_rng([zlib.crc32(name.encode()), seed]).standard_normal(out[name].shape)
        drawn = base * np.exp(spread * noise) if base else spread * noise
        out[name] = jnp.asarray(drawn.astype(out[name].dtype))
    for name, factor in factors.items():
        out[name] = (out[name] * factor).astype(out[name].dtype)
    return out
```

```python
from contextlib import ExitStack

import concourse.bass as bass
from concourse import mybir

F32 = mybir.dt.float32
BF16 = mybir.dt.bfloat16
I32 = mybir.dt.int32
ALU = mybir.AluOpType
ACT = mybir.ActivationFunctionType
AX = mybir.AxisListType

P = 128
B, T, D = 16, 256, 256
H, HD, E = 16, 16, 8
F = 1024
NT = T // P
DC = D // P
FC = F // P
LANES = 2
TURNS = B // LANES
G = 2
HG = H // G
QH = 4
VW = 32
SCALE = HD ** -0.5
EPS = 1e-5
MASKED = -1e12
FUTURE = -3e38
PRODUCTS = 6 * HD
BIAS = PRODUCTS + 3
ROWS = BIAS + 3
Q_PARTS = [0, 1, 2, 0, 1, 0]
K_PARTS = [0, 1, 0, 1, 0, 2]
EXPS = 10
UNITS = ("l0 cross", "l0 self", "l1 joint", "l1 causal")


def lane_steps(l):
    out = []
    for u in range(4):
        srcs = 2 if u == 2 else 1
        pre = [("LN", l, u, 0), ("XT", l, u, 0)]
        if u == 0:
            pre = [("LOAD", l, u, 0)] + pre + [("KT", l, u, 0), ("SPLIT", l, u, 0), ("STACKW", l, u, 0), ("STACKR", l, u, 0)]
        else:
            pre += [("Q", l, u, 0), ("K", l, u, 0), ("SPLIT", l, u, 0), ("STACKW", l, u, 0), ("V", l, u, 0), ("STACKR", l, u, 0)]
        if u == 1:
            pre += [("UNBIAS", l, u, 0), ("GATE", l, u, 0), ("GEXP", l, u, 0)]
        out += pre
        fill = []
        if u == 1:
            fill = [("TOP", l, u, 0), ("CT", l, u, 0), ("MBIAS", l, u, 0)]
            fill += [("EXPERT", l, u, (t, e)) for t in range(NT) for e in range(0, E, 2)]
        body = []
        for g in range(G):
            slots = [("S", l, u, (h, s)) for h in range(g * HG, (g + 1) * HG) for s in range(srcs)]
            for k, s in enumerate(slots):
                body.append(s)
                if g and k == 1:
                    body.append(("MT", l, u, g - 1))
            body.append(("M", l, u, g))
        late = []
        for g in range(G):
            slots = [("T", l, u, (h, s)) for h in range(g * HG, (g + 1) * HG) for s in range(srcs)]
            for k, s in enumerate(slots):
                body.append(s)
                if g == 0 and k == 1:
                    body.append(("MT", l, u, G - 1))
                late = [(n - 1, x) for n, x in late]
                body += [x for n, x in late if n == 0]
                late = [(n, x) for n, x in late if n > 0]
                if (k + 1) % (QH * srcs) == 0:
                    q = (g * HG + k // srcs) // QH
                    late += [(2, ("PV", l, u, q)), (4, ("OT", l, u, q))]
        body += [x for n, x in late]
        every = max(1, len(body) // (len(fill) + 1))
        for k, s in enumerate(body):
            out.append(s)
            if fill and k % every == every - 1:
                out.append(fill.pop(0))
        out += fill
        if u >= 2:
            out += [("OTT", l, u, 0), ("PROJ", l, u, 0)]
    out += [("LNH", l, 3, 0), ("HT", l, 3, 0), ("GATE", l, 3, 0), ("GEXP", l, 3, 0), ("TOP", l, 3, 0), ("STORE", l, 3, 0)]
    return out


LAG = 0.11


def merged_steps():
    at = []
    for l in range(LANES):
        steps = lane_steps(l)
        at += [((k + 0.5) / len(steps) + l * LAG, l, k, s) for k, s in enumerate(steps)]
    return [s for *_, s in sorted(at)]


STEPS = merged_steps()
PRE = ("XT", "KT", "Q", "K", "V", "GATE", "CT", "MBIAS", "EXPERT", "OTT", "PROJ", "HT")


def numbered(keys):
    return {k: n for n, k in enumerate(keys)}


S_AT = numbered(s for s in STEPS if s[0] == "S")
T_AT = numbered(s for s in STEPS if s[0] == "T")
EX_AT = {}
for _l in range(LANES):
    EX_AT.update(numbered(s for s in STEPS if s[0] == "T" and s[1] == _l))
M_AT = numbered(s for s in STEPS if s[0] == "M")
PV_AT = numbered(s for s in STEPS if s[0] == "PV")
TR_AT = numbered(s for s in STEPS if s[0] in ("MT", "OT"))
PRE_AT = {}
for _l in range(LANES):
    PRE_AT.update(numbered(s for s in STEPS if s[0] in PRE and s[1] == _l))
N_S, N_T, N_M, N_PV, N_TR = len(S_AT), len(T_AT), len(M_AT), len(PV_AT), len(TR_AT)
N_PRE = len(PRE_AT) // LANES
POOL_OF = {"LOAD": 1, "SPLIT": 4, "UNBIAS": 1}
POOL_AT, POOL_STEPS = {}, 0
for _s in STEPS:
    if _s[0] in POOL_OF:
        POOL_STEPS += POOL_OF[_s[0]]
        POOL_AT[_s] = POOL_STEPS


class Steps:

    def __init__(self, eng, sem, turn=0, per_turn=0, passed=None, before=0):
        self.eng, self.sem, self.base, self.n, self.passed = eng, sem, turn * per_turn + before, 0, passed

    def done(self, ins):
        ins.then_inc(self.sem, 1)
        self.n += 1

    def wait(self):
        self.eng.wait_ge(self.sem, self.base + self.n)

    def wait_alone(self):
        self.wait()
        self.stand()

    def stand(self):
        self.eng.sem_inc(self.passed, 1)


NEWTON = 3
RSQRT_GUESS = 0x5F3759DF
DVE_STEPS = 380
FFN_STEPS = 40


def inverse_root(dve, s, var, out, v, w):
    s.done(dve.tensor_scalar(v, var, EPS, None, ALU.add))
    s.wait()
    s.done(dve.tensor_scalar(out.bitcast(I32), v.bitcast(I32), 1, None, ALU.logical_shift_right))
    s.wait()
    s.done(dve.tensor_scalar(out.bitcast(I32), out.bitcast(I32), -1.0, float(RSQRT_GUESS), ALU.mult, ALU.add))
    s.wait()
    for _ in range(NEWTON):
        s.done(dve.tensor_tensor(w, out, out, ALU.mult))
        s.wait()
        s.done(dve.scalar_tensor_tensor(out=w, in0=w, scalar=-0.5, in1=v, op0=ALU.mult, op1=ALU.mult))
        s.wait()
        s.done(dve.scalar_tensor_tensor(out=out, in0=w, scalar=1.5, in1=out, op0=ALU.add, op1=ALU.mult))
        s.wait()


def build(nc, x, ctx_in, itok, g_xattn, g_ffn, key_b, w0_qkv, b0_qkv, w0_gate, b0_gate, w0_exp, b0_exp,
          w1x_qkv, w1x_proj, b1x_proj, w1_qkv, w1_o, ln1_g, ln1_b, w1_gate, w_up, b_up, w_down, b_down,
          ln2_g, ln2_b, out):
    dram = lambda name, shape, dt: nc.dram_tensor(name, shape, dt, kind="Internal").ap()
    bias_d = dram("key_bias_parts", [B, 3, T], BF16)
    q_d = [dram(f"q_parts_{l}", [3, HD, H, T], BF16) for l in range(LANES)]
    k_d = [dram(f"k_parts_{l}", [3, HD, H, T], BF16) for l in range(LANES)]
    x3_d = dram("x3", [B, P, NT, D], F32)
    h_d = dram("h", [B, P, NT, D], F32)
    ht_d = dram("h_transposed", [B, P, DC, T], F32)
    c_d = dram("combine", [B, P, NT, E], F32)
    keep = ExitStack()
    with keep:
        tanh_g = keep.enter_context(nc.sbuf_tensor("tanh_g", [P, 4], F32))
        ident = keep.enter_context(nc.sbuf_tensor("ident", [P, P], F32))
        attention_phase(nc, locals())
        expert_phase(nc, locals())


def attention_phase(nc, a):
    x, ctx_in, tanh_g, ident = a["x"], a["ctx_in"], a["tanh_g"], a["ident"]
    bias_d, q_d, k_d = a["bias_d"], a["q_d"], a["k_d"]
    own = ExitStack()
    with own:
        sb = lambda name, shape, dt=F32: own.enter_context(nc.sbuf_tensor(name, shape, dt))
        sem = lambda name: own.enter_context(nc.semaphore(name))
        lanes = range(LANES)
        lsb = lambda name, shape, dt=F32: [sb(f"{name}{l}", shape, dt) for l in lanes]
        lsem = lambda name: [sem(f"{name}{l}") for l in lanes]
        w0 = sb("w0", [P, DC, 3 * D]); w1x = sb("w1x", [P, DC, 3 * D]); w1 = sb("w1", [P, DC, 3 * D])
        wproj = sb("wproj", [P, DC, D]); wo = sb("wo", [P, DC, D])
        wexp = sb("wexp", [P, DC, E, D]); bexp = sb("bexp", [E, D])
        wg0 = sb("wg0", [P, DC, E]); wg1 = sb("wg1", [P, DC, E]); bg0 = sb("bg0", [P, E])
        bqk = sb("bqk", [P, 4]); bv = sb("bv", [P, D]); bproj = sb("bproj", [P, D])
        g1 = sb("g1", [P, D]); b1 = sb("b1", [P, D])
        ident_b = sb("ident_b", [P, P], BF16)
        late_k = sb("late_k", [P, P], BF16)
        late_q = sb("late_q", [P, P], BF16)
        first = sb("first", [P, NT, E])
        xs = lsb("xs", [P, NT, D]); ctx = lsb("ctx", [P, NT, 2 * D])
        xn = lsb("xn", [P, NT, D]); xt = lsb("xt", [P, DC, T])
        aq = lsb("aq", [P, DC, T]); ak = lsb("ak", [P, DC, T])
        pq = lsb("pq", [P, 3, DC, T], BF16); pk = lsb("pk", [P, 3, DC, T], BF16)
        qs = lsb("qs", [ROWS, H, T], BF16); ks = lsb("ks", [ROWS, H, T], BF16); kc = lsb("kc", [ROWS, H, T], BF16)
        va = lsb("va", [P, NT, H, VW]); vc = lsb("vc", [P, NT, H, VW])
        mx = lsb("mx", [P, H, 2]); mx3 = lsb("mx3", [P, H, 3])
        mr = sb("mr", [P, NT, HG]); mp = [[sb(f"mp{l}{g}", [P, NT, 3, HG], BF16) for g in range(G)] for l in lanes]
        mt = [[sb(f"mt{l}{g}", [3 * HG, T], BF16) for g in range(G)] for l in lanes]
        ex = lsb("ex", [P, EXPS, 2 * T])
        ot = [sb(f"ot{k}", [P, T]) for k in range(2)]
        rden = sb("rden", [P, NT, QH])
        o = lsb("o", [P, NT, D]); moe = lsb("moe", [P, NT, D])
        stats = lsb("stats", [P, NT, 6]); mv = lsb("mv", [P, NT, 2]); rstd = lsb("rstd", [P, NT])
        root_v = sb("root_v", [P, NT]); root_w = sb("root_w", [P, NT])
        lg = lsb("lg", [P, NT, E]); pr = lsb("pr", [P, NT, E]); comb = lsb("comb", [P, NT, E])
        t8 = [lsb(f"t8_{k}_", [P, NT, E]) for k in range(3)]
        t1 = [lsb(f"t1_{k}_", [P, NT]) for k in range(4)]
        combt = lsb("combt", [E, T])
        lens = sb("lens", [B, 1], I32); lenf = sb("lenf", [B, 1])
        keyi = xs[0][0:B, 0, :].bitcast(I32); kbf = xs[0][0:B, 1, :]; kbb = xs[1][0:B, 0, :]; kbp = pq[0][0:B, :, 0, :]

        ps = lambda name: own.enter_context(nc.psum_tensor(name, [P, 512], F32))
        s_ps = [ps(f"s_ps{k}") for k in range(2)]
        t_ps = [ps(f"t_ps{k}") for k in range(2)]
        pv_ps = ps("pv_ps")
        tr_ps = ps("tr_ps")
        pre_ps = [ps(f"pre_ps{l}") for l in lanes]
        tr_b = tr_ps[:, :].bitcast(BF16)

        w_loaded, small_loaded, raw_loaded, itok_loaded = sem("w_loaded"), sem("small_loaded"), sem("raw_loaded"), sem("itok_loaded")
        consts_ready, setup_step, bias_ready, bias_stored = sem("consts_ready"), sem("setup_step"), sem("bias_ready"), sem("bias_stored")
        raw_turned, raw_copied, tanh_ready, pool_setup = sem("raw_turned"), sem("raw_copied"), sem("tanh_ready"), sem("pool_setup")
        x_loaded, xn_ready = lsem("x_loaded"), lsem("xn_ready")
        pre_ready, pre_read = lsem("pre_ready"), lsem("pre_read")
        q_split, q_stored, k_stored = lsem("q_split"), lsem("q_stored"), lsem("k_stored")
        q_rows, k_rows, max_rows = lsem("q_rows"), lsem("k_rows"), lsem("max_rows")
        s_ready, s_read, t_ready, t_read = sem("s_ready"), sem("s_read"), sem("t_ready"), sem("t_read")
        m_ready, tr_ready, tr_read, pv_ready, pv_read = sem("m_ready"), sem("tr_ready"), sem("tr_read"), sem("pv_ready"), sem("pv_read")
        lg_ready, lg_exp, top_done, h_ready, stored = lsem("lg_ready"), lsem("lg_exp"), lsem("top_done"), lsem("h_ready"), lsem("stored")
        dve_step, pool_done, dve_passed, pool_passed = sem("dve_step"), sem("pool_done"), sem("dve_passed"), sem("pool_passed")

        W_DMAS, SMALL_DMAS, RAW_DMAS, STORES = 9, 10, 2, 4
        raw = ex[0][:, :, :].rearrange("p a b -> p (a b)")[:, 0:8 * D].rearrange("p (r n) -> p r n", n=D)

        with nc.Block() as block:
            @block.sync
            def _(sp):
                sp.dma_start(lens[:, :], a["itok"]).then_inc(itok_loaded, 16)
                sp.dma_start(kbb[:, :], a["key_b"].partition_broadcast(B)).then_inc(itok_loaded, 16)
                sp.dma_start(raw[:, 0:6, :], a["w1x_qkv"].rearrange("(r p) n -> p r n", p=P)).then_inc(raw_loaded, 16)
                sp.dma_start(raw[:, 6:8, :], a["w1x_proj"].rearrange("(r p) n -> p r n", p=P)).then_inc(raw_loaded, 16)
                sp.dma_start(tanh_g[:, 0:2], a["g_xattn"].partition_broadcast(P)).then_inc(small_loaded, 16)
                sp.dma_start(tanh_g[:, 2:4], a["g_ffn"].partition_broadcast(P)).then_inc(small_loaded, 16)
                sp.dma_start(bqk[:, :], a["b0_qkv"][0:2 * D].rearrange("(c p) -> p c", p=P), allow_slow_non_contiguous=True).then_inc(small_loaded, 16)
                sp.dma_start(bv[:, :], a["b0_qkv"][2 * D:3 * D].partition_broadcast(P)).then_inc(small_loaded, 16)
                sp.dma_start(bg0[:, :], a["b0_gate"].partition_broadcast(P)).then_inc(small_loaded, 16)
                sp.dma_start(bproj[:, :], a["b1x_proj"].partition_broadcast(P)).then_inc(small_loaded, 16)
                sp.dma_start(g1[:, :], a["ln1_g"].partition_broadcast(P)).then_inc(small_loaded, 16)
                sp.dma_start(b1[:, :], a["ln1_b"].partition_broadcast(P)).then_inc(small_loaded, 16)
                sp.dma_start(bexp[:, :], a["b0_exp"]).then_inc(small_loaded, 16)
                sp.dma_start(wg0[:, :, :], a["w0_gate"].rearrange("(c p) n -> p c n", p=P)).then_inc(small_loaded, 16)
                chunked = lambda w: w.rearrange("(c p) n -> p c n", p=P)
                sp.dma_start(wg1[:, :, :], chunked(a["w1_gate"])).then_inc(w_loaded, 16)
                sp.dma_start(w0[:, :, :], chunked(a["w0_qkv"])).then_inc(w_loaded, 16)
                for c in range(DC):
                    sp.dma_start(wexp[:, c, :, :], a["w0_exp"][:, c * P:(c + 1) * P, :].rearrange("e p n -> p e n")).then_inc(w_loaded, 16)
                sp.dma_start(w1[:, :, :], chunked(a["w1_qkv"])).then_inc(w_loaded, 16)
                sp.dma_start(wo[:, :, :], chunked(a["w1_o"])).then_inc(w_loaded, 16)
                sp.wait_ge(bias_ready, 1)
                sp.dma_start(bias_d, kbp[:, :, :]).then_inc(bias_stored, 16)
                sp.wait_ge(bias_stored, 16)
                sp.wait_ge(w_loaded, 16 * (W_DMAS - 3))
                for l in lanes:
                    sp.sem_inc(stored[l], 16 * STORES)

            @block.gpsimd
            def _(pool):
                pool.memset(ident[:, :], 0.0).then_inc(pool_setup, 1)
                pool.memset(late_k[:, :], 0.0).then_inc(pool_setup, 1)
                pool.memset(late_q[:, :], 0.0).then_inc(pool_setup, 1)
                pool.wait_ge(pool_setup, 3)
                pool.affine_select(out=ident[:, :], in_=ident[:, :], compare_op=ALU.not_equal, fill=1.0, base=0,
                                   pattern=[[-1, P]], channel_multiplier=1).then_inc(pool_setup, 1)
                pool.affine_select(out=late_k[:, :], in_=late_k[:, :], compare_op=ALU.is_ge, fill=FUTURE, base=0,
                                   pattern=[[-1, P]], channel_multiplier=1).then_inc(pool_setup, 1)
                pool.affine_select(out=late_q[:, :], in_=late_q[:, :], compare_op=ALU.is_ge, fill=FUTURE, base=0,
                                   pattern=[[1, P]], channel_multiplier=-1).then_inc(pool_setup, 1)
                pool.iota(keyi[:, :], pattern=[[1, T]], base=0, channel_multiplier=0).then_inc(pool_setup, 1)
                pool.wait_ge(pool_setup, 4)
                pool.tensor_copy(ident_b[:, :], ident[:, :]).then_inc(consts_ready, 1)
                for l in lanes:
                    for v in (va[l], vc[l]):
                        pool.memset(v[:, :, :, :], 0.0).then_inc(pool_setup, 1)
                pool.wait_ge(pool_setup, 7 + 2 * LANES)
                pool.sem_inc(pool_done, 1)
                for l in lanes:
                    for v in (va[l], vc[l]):
                        pool.memset(v[:, :, :, HD:HD + 1], 1.0).then_inc(consts_ready, 1)

            @block.vector
            def _(dve):
                s = Steps(dve, setup_step)
                for l in lanes:
                    s.done(dve.memset(qs[l][PRODUCTS:ROWS, :, :], 1.0))
                    s.done(dve.memset(ks[l][PRODUCTS:ROWS, :, :], 1.0))
                    s.done(dve.memset(kc[l][PRODUCTS:ROWS, :, :], 1.0))
                for k in range(E):
                    s.done(dve.memset(first[:, :, k:k + 1], float(E - k)))
                s.wait()
                for l in lanes:
                    s.done(dve.memset(ks[l][PRODUCTS:BIAS, :, :], 0.0))
                dve.wait_ge(itok_loaded, 32)
                dve.wait_ge(pool_setup, 7)
                s.done(dve.tensor_copy(lenf[:, :], lens[:, :]))
                s.done(dve.tensor_copy(kbf[:, :], keyi[:, :]))
                s.wait()
                s.done(dve.tensor_scalar(kbf[:, :], kbf[:, :], lenf[:, 0:1], 1.0, ALU.is_lt, ALU.subtract))
                s.wait()
                s.done(dve.scalar_tensor_tensor(out=kbf[:, :], in0=kbf[:, :], scalar=-MASKED, in1=kbb[:, :], op0=ALU.mult, op1=ALU.add))
                s.wait()
                s.done(dve.tensor_copy(kbp[:, 0, :], kbf[:, :]))
                s.wait()
                s.done(dve.tensor_tensor(kbf[:, :], kbf[:, :], kbp[:, 0, :], ALU.subtract))
                s.wait()
                s.done(dve.tensor_copy(kbp[:, 1, :], kbf[:, :]))
                s.wait()
                dve.tensor_tensor(kbp[:, 2, :], kbf[:, :], kbp[:, 1, :], ALU.subtract).then_inc(bias_ready, 1)
                dve.wait_ge(small_loaded, 16 * SMALL_DMAS)
                s.done(dve.tensor_scalar(bqk[:, 0:2], bqk[:, 0:2], SCALE, None, ALU.mult))
                dve.wait_ge(tanh_ready, 1)
                s.done(dve.tensor_scalar(bproj[:, :], bproj[:, :], tanh_g[:, 1:2], None, ALU.mult))
                for k in range(8):
                    dve.wait_ge(raw_turned, k + 1)
                    dst = w1x[:, :, k * P:(k + 1) * P] if k < 6 else wproj[:, :, (k - 6) * P:(k - 5) * P]
                    dve.tensor_copy(dst, s_ps[k % 2][:, 0:D].rearrange("p (c n) -> p c n", c=DC)).then_inc(raw_copied, 1)
                s.wait()
                dve.sem_inc(s_read, 2)
                dve.sem_inc(tr_read, 1)
                for l in lanes:
                    dve.sem_inc(pre_read[l], 1)

            @block.scalar
            def _(act):
                act.wait_ge(small_loaded, 16 * SMALL_DMAS)
                act.activation(tanh_g[:, :], tanh_g[:, :], ACT.Tanh).then_inc(tanh_ready, 1)
                act.sem_inc(t_read, 2)
                act.sem_inc(pv_read, 1)

            @block.tensor
            def _(pe):
                pe.wait_ge(raw_loaded, 16 * RAW_DMAS)
                pe.wait_ge(pool_setup, 4)
                for k in range(8):
                    if k >= 2:
                        pe.wait_ge(raw_copied, k - 1)
                    for c in range(DC):
                        last = pe.transpose(s_ps[k % 2][:, c * P:(c + 1) * P], raw[:, k, c * P:(c + 1) * P], ident[:, :])
                    last.then_inc(raw_turned, 1)

        def o_done(l, u):
            return TR_AT[("OT", l, u, H // QH - 1)] + 2

        def pre_done(step):
            return PRE_AT[step] + 2

        with nc.Block() as block:
            @block.sync
            def _(sp):
                with sp.Fori(0, TURNS) as it:
                    batch = [sp.snap(it * LANES + l) for l in lanes]

                    def wait_all(*pairs):
                        values = [sp.snap(v) for _, v in pairs]
                        for (s, _), v in zip(pairs, values):
                            sp.wait_ge(s, v)

                    for name, l, u, k in STEPS:
                        if name == "LOAD":
                            one = lambda d: d[bass.ds(batch[l], 1)]
                            wait_all((stored[l], it * 16 * STORES + 16 * STORES))
                            sp.dma_start(xs[l][:, :, :], one(x).rearrange("o (t p) d -> p (o t) d", p=P)).then_inc(x_loaded[l], 16)
                            sp.dma_start(ctx[l][:, :, :], one(ctx_in).rearrange("o (t p) d -> p (o t) d", p=P)).then_inc(x_loaded[l], 16)
                            for part in range(3):
                                row = one(bias_d)[:, part, :].unsqueeze(1).broadcast_to([1, H, T])
                                sp.dma_start(kc[l][PRODUCTS + part:PRODUCTS + part + 1, :, :], row).then_inc(x_loaded[l], 16)
                        if name == "STACKW":
                            split = it * POOL_STEPS + POOL_AT[("SPLIT", l, u, 0)] + 1
                            for parts, ready, value, dst, done in ((pq[l], q_split[l], it * 4 + u + 1, q_d[l], q_stored[l]),
                                                                   (pk[l], pool_done, split, k_d[l], k_stored[l])):
                                wait_all((ready, value))
                                for part in range(3):
                                    for c in range(DC):
                                        sp.dma_start(dst[part, :, c * 8:(c + 1) * 8, :].rearrange("d h t -> h d t"),
                                                     parts[:, part, c, :]).then_inc(done, 16)
                        if name == "STACKR":
                            kst = kc if u == 0 else ks
                            for order, src, stored_, dst, done in ((Q_PARTS, q_d[l], q_stored[l], qs[l], q_rows[l]),
                                                                   (K_PARTS, k_d[l], k_stored[l], kst[l], k_rows[l])):
                                wait_all((stored_, it * 4 * 96 + (u + 1) * 96))
                                for r, part in enumerate(order):
                                    sp.dma_start(dst[r * HD:(r + 1) * HD, :, :], src[part]).then_inc(done, 16)
                        if name == "MT":
                            r = TR_AT[(name, l, u, k)]
                            wait_all((tr_read, it * N_TR + r + 2))
                            for part in range(3):
                                sp.dma_start(qs[l][BIAS + part:BIAS + part + 1, k * HG:(k + 1) * HG, :],
                                             mt[l][k][part * HG:(part + 1) * HG, :]).then_inc(max_rows[l], 16)
                        if name == "STORE":
                            one = lambda d: d[bass.ds(batch[l], 1)].rearrange("o p t n -> p (o t) n")
                            wait_all((top_done[l], it * 2 + 2))
                            sp.dma_start(one(a["x3_d"]), xs[l][:, :, :]).then_inc(stored[l], 16)
                            sp.dma_start(one(a["h_d"]), moe[l][:, :, :]).then_inc(stored[l], 16)
                            sp.dma_start(one(a["ht_d"]), xt[l][:, :, :]).then_inc(stored[l], 16)
                            sp.dma_start(one(a["c_d"]), comb[l][:, :, :]).then_inc(stored[l], 16)
                for l in lanes:
                    sp.wait_ge(stored[l], 16 * STORES * (TURNS + 1))

            @block.tensor
            def _(pe):
                nc.disable_value_cache = True
                with pe.Fori(0, TURNS) as it:
                    def begin_pre(step):
                        pe.wait_ge(pre_read[step[1]], it * N_PRE + PRE_AT[step] + 1)

                    def turn_tokens(dst, src):
                        for c in range(DC):
                            for t in range(NT):
                                last = pe.transpose(dst[:, c * T + t * P:c * T + (t + 1) * P], src[:, t, c * P:(c + 1) * P], ident[:, :])
                        return last

                    def project_t(dst, w, at, src):
                        for half in range(DC):
                            for c in range(DC):
                                last = pe.matmul(dst[:, half * T:(half + 1) * T], w[:, c, at + half * P:at + (half + 1) * P],
                                                 src[:, c, :], start=c == 0, stop=c == DC - 1)
                        return last

                    def project(dst, w, src, n):
                        for t in range(NT):
                            for c in range(DC):
                                last = pe.matmul(dst[:, t * n:(t + 1) * n], src[:, c, t * P:(t + 1) * P], w[:, c, :],
                                                 start=c == 0, stop=c == DC - 1)
                        return last

                    for step in STEPS:
                        name, l, u, k = step
                        bank = pre_ps[l]
                        w_of = (None, w0, w1x, w1)[u]
                        if name == "XT":
                            pe.wait_ge(xn_ready[l], it * 4 + u + 1)
                            begin_pre(step)
                            turn_tokens(bank, xn[l]).then_inc(pre_ready[l], 1)
                        elif name == "KT":
                            pe.wait_ge(x_loaded[l], it * 80 + 80)
                            begin_pre(step)
                            turn_tokens(bank, ctx[l]).then_inc(pre_ready[l], 1)
                        elif name in ("Q", "K"):
                            begin_pre(step)
                            project_t(bank, w_of, 0 if name == "Q" else D, xt[l]).then_inc(pre_ready[l], 1)
                        elif name == "V":
                            begin_pre(step)
                            project(bank, w_of[:, :, 2 * D:3 * D], xt[l], D).then_inc(pre_ready[l], 1)
                        elif name == "GATE":
                            begin_pre(step)
                            project(bank, wg0 if u == 1 else wg1, xt[l], E).then_inc(pre_ready[l], 1)
                        elif name == "CT":
                            pe.wait_ge(top_done[l], it * 2 + 1)
                            begin_pre(step)
                            for t in range(NT):
                                last = pe.transpose(bank[0:E, t * P:(t + 1) * P], comb[l][:, t, :], ident[:, :])
                            last.then_inc(pre_ready[l], 1)
                        elif name == "MBIAS":
                            begin_pre(step)
                            for t in range(NT):
                                last = pe.matmul(bank[:, t * D:(t + 1) * D], combt[l][:, t * P:(t + 1) * P], bexp[:, :], start=True, stop=True)
                            last.then_inc(pre_ready[l], 1)
                        elif name == "EXPERT":
                            t, e = k
                            begin_pre(step)
                            for c in range(DC):
                                last = pe.matmul(bank[:, :], xt[l][:, c, t * P:(t + 1) * P],
                                                 wexp[:, c, e:e + 2, :].rearrange("p e n -> p (e n)"), start=c == 0, stop=c == DC - 1)
                            last.then_inc(pre_ready[l], 1)
                        elif name == "OTT":
                            pe.wait_ge(tr_read, it * N_TR + o_done(l, u))
                            begin_pre(step)
                            turn_tokens(bank, o[l]).then_inc(pre_ready[l], 1)
                        elif name == "PROJ":
                            begin_pre(step)
                            project(bank, wproj if u == 2 else wo, xt[l], D).then_inc(pre_ready[l], 1)
                        elif name == "HT":
                            pe.wait_ge(h_ready[l], it + 1)
                            begin_pre(step)
                            turn_tokens(bank, moe[l]).then_inc(pre_ready[l], 1)
                        elif name == "S":
                            n = S_AT[step]
                            h, src = k
                            if h == 0 and src == 0:
                                pe.wait_ge(q_rows[l], it * 4 * 96 + (u + 1) * 96)
                                pe.wait_ge(k_rows[l], it * 4 * 96 + (u + 1) * 96)
                            pe.wait_ge(s_read, it * N_S + n + 1)
                            dst = s_ps[n % 2]
                            rows = BIAS if u == 0 else PRODUCTS
                            q = lambda t: qs[l][0:rows, h, t * P:(t + 1) * P]
                            if u == 2:
                                pe.matmul(dst[:, 0:T], q(src), kc[l][0:rows, h, :], start=True, stop=True)
                                last = pe.matmul(dst[:, T:2 * T], q(src), ks[l][0:rows, h, :], start=True, stop=True)
                            elif u == 3:
                                pe.matmul(dst[:, 0:P], q(0), ks[l][0:rows, h, 0:P], start=True, stop=False)
                                pe.matmul(dst[:, 0:P], ident_b[:, :], late_k[:, :], start=False, stop=True)
                                pe.matmul(dst[:, P:3 * P], q(1), ks[l][0:rows, h, :], start=True, stop=False)
                                last = pe.matmul(dst[:, 2 * P:3 * P], ident_b[:, :], late_k[:, :], start=False, stop=True)
                            else:
                                kst = kc[l] if u == 0 else ks[l]
                                for t in range(NT):
                                    last = pe.matmul(dst[:, t * T:(t + 1) * T], q(t), kst[0:rows, h, :], start=True, stop=True)
                            last.then_inc(s_ready, 1)
                        elif name == "MT":
                            pe.wait_ge(m_ready, it * N_M + M_AT[("M", l, u, k)] + 1)
                            pe.wait_ge(tr_read, it * N_TR + TR_AT[step] + 1)
                            for t in range(NT):
                                last = pe.transpose(tr_b[0:3 * HG, t * P:(t + 1) * P],
                                                    mp[l][k][:, t, :, :].rearrange("p a b -> p (a b)"), ident_b[:, :])
                            last.then_inc(tr_ready, 1)
                        elif name == "T":
                            n = T_AT[step]
                            h, src = k
                            if h % HG == 0 and src == 0:
                                pe.wait_ge(max_rows[l], it * 4 * G * 48 + (u * G + h // HG + 1) * 48)
                                if u == 2 and h == 0:
                                    pe.wait_ge(pool_done, it * POOL_STEPS + POOL_AT[("UNBIAS", l, 1, 0)] + 1)
                            pe.wait_ge(t_read, it * N_T + n + 1)
                            dst = t_ps[n % 2]
                            kst = kc[l] if u == 0 or (u == 2 and src == 0) else ks[l]
                            if u == 3:
                                pe.matmul(dst[:, 0:T], kst[0:ROWS, h, 0:P], qs[l][0:ROWS, h, :], start=True, stop=False)
                                pe.matmul(dst[:, 0:P], ident_b[:, :], late_q[:, :], start=False, stop=True)
                                pe.matmul(dst[:, T:T + P], kst[0:ROWS, h, P:T], qs[l][0:ROWS, h, P:T], start=True, stop=False)
                                last = pe.matmul(dst[:, T:T + P], ident_b[:, :], late_q[:, :], start=False, stop=True)
                            else:
                                for t in range(NT):
                                    last = pe.matmul(dst[:, t * T:(t + 1) * T], kst[0:ROWS, h, t * P:(t + 1) * P],
                                                     qs[l][0:ROWS, h, :], start=True, stop=True)
                            last.then_inc(t_ready, 1)
                        elif name == "PV":
                            v = PV_AT[step]
                            srcs = 2 if u == 2 else 1
                            slots = {(j, s): ("T", l, u, (k * QH + j, s)) for j in range(QH) for s in range(srcs)}
                            pe.wait_ge(t_read, it * N_T + max(T_AT[s] for s in slots.values()) + 3)
                            if k == 0:
                                if u in (0, 2):
                                    pe.wait_ge(pool_done, it * POOL_STEPS + POOL_AT[("LOAD", l, 0, 0)] + 1)
                                if u:
                                    pe.wait_ge(pre_read[l], it * N_PRE + pre_done(("V", l, u, 0)))
                            pe.wait_ge(pv_read, it * N_PV + v + 1)
                            for s in range(srcs):
                                val = vc[l] if u == 0 or (u == 2 and s == 0) else va[l]
                                for t in range(NT):
                                    q0 = P if u == 3 and t == 1 else 0
                                    for j in range(QH):
                                        e = ex[l][:, EX_AT[slots[(j, s)]] % EXPS, t * T:t * T + T - q0]
                                        last = pe.matmul(pv_ps[j * VW:(j + 1) * VW, q0:T], val[:, t, k * QH + j, :], e,
                                                         start=s == 0 and t == 0, stop=s == srcs - 1 and t == NT - 1,
                                                         tile_position=(0, j * VW))
                            last.then_inc(pv_ready, 1)
                        elif name == "OT":
                            v = PV_AT[("PV", l, u, k)]
                            pe.wait_ge(pv_read, it * N_PV + v + 2)
                            pe.wait_ge(tr_read, it * N_TR + TR_AT[step] + 1)
                            for t in range(NT):
                                last = pe.transpose(tr_ps[:, t * P:(t + 1) * P], ot[v % 2][:, t * P:(t + 1) * P], ident[:, :])
                            last.then_inc(tr_ready, 1)

            @block.scalar
            def _(act):
                with act.Fori(0, TURNS) as it:
                    def produced(step):
                        act.wait_ge(pre_ready[step[1]], it * N_PRE + PRE_AT[step] + 1)

                    for step in STEPS:
                        name, l, u, k = step
                        bank = pre_ps[l]
                        flat = lambda z: z[:, :, :].rearrange("p a b -> p (a b)")
                        if name in ("XT", "KT", "OTT", "HT"):
                            produced(step)
                            dst = ak[l] if name == "KT" else aq[l] if u == 0 else xt[l]
                            by = SCALE if name == "XT" and u == 0 else 1.0
                            act.activation(flat(dst), bank[:, :], ACT.Copy, scale=by).then_inc(pre_read[l], 1)
                        elif name in ("Q", "K"):
                            produced(step)
                            dst = aq[l] if name == "Q" else ak[l]
                            by = SCALE if name == "Q" else 1.0
                            if u == 1:
                                for c in range(DC):
                                    col = c if name == "Q" else DC + c
                                    last = act.activation(dst[:, c, :], bank[:, c * T:(c + 1) * T], ACT.Identity,
                                                          bias=bqk[:, col:col + 1], scale=by)
                            else:
                                last = act.activation(flat(dst), bank[:, :], ACT.Copy, scale=by)
                            last.then_inc(pre_read[l], 1)
                        elif name == "V" and u > 1:
                            produced(step)
                            act.activation(va[l][:, :, :, 0:HD], bank[:, :].rearrange("p (t h d) -> p t h d", t=NT, h=H),
                                           ACT.Copy).then_inc(pre_read[l], 1)
                        elif name == "CT":
                            produced(step)
                            act.activation(combt[l][:, :], bank[0:E, 0:T], ACT.Copy).then_inc(pre_read[l], 1)
                        elif name == "GEXP":
                            act.wait_ge(lg_ready[l], it * 2 + (u == 3) + 1)
                            act.activation(flat(pr[l]), flat(lg[l]), ACT.Exp).then_inc(lg_exp[l], 1)
                        elif name == "MT":
                            act.wait_ge(tr_ready, it * N_TR + TR_AT[step] + 1)
                            act.activation(mt[l][k][:, :], tr_b[0:3 * HG, 0:T], ACT.Copy).then_inc(tr_read, 1)
                        elif name == "T":
                            n = T_AT[step]
                            act.wait_ge(t_ready, it * N_T + n + 1)
                            w = 3 * P if u == 3 else 2 * T
                            act.activation(ex[l][:, EX_AT[step] % EXPS, 0:w], t_ps[n % 2][:, 0:w], ACT.Exp).then_inc(t_read, 1)
                        elif name == "PV":
                            v = PV_AT[step]
                            act.wait_ge(pv_ready, it * N_PV + v + 1)
                            act.activation(ot[v % 2][:, :], pv_ps[:, 0:T], ACT.Copy).then_inc(pv_read, 1)

            @block.gpsimd
            def _(pool):
                with pool.Fori(0, TURNS) as it:
                    s = Steps(pool, pool_done, it, POOL_STEPS, pool_passed, 1)
                    for step in STEPS:
                        name, l, u, k = step
                        if name == "LOAD":
                            pool.wait_ge(x_loaded[l], it * 80 + 80)
                            s.wait_alone()
                            s.done(pool.tensor_copy(vc[l][:, :, :, 0:HD], ctx[l][:, :, D:2 * D].rearrange("p t (h d) -> p t h d", h=H)))
                        elif name == "SPLIT":
                            pool.wait_ge(pre_read[l], it * N_PRE + pre_done(("KT" if u == 0 else "K", l, u, 0)))
                            s.wait_alone()
                            s.done(pool.tensor_copy(pk[l][:, 0, :, :], ak[l][:, :, :]))
                            s.wait()
                            s.done(pool.tensor_tensor(ak[l][:, :, :], ak[l][:, :, :], pk[l][:, 0, :, :], ALU.subtract))
                            s.wait_alone()
                            s.done(pool.tensor_copy(pk[l][:, 1, :, :], ak[l][:, :, :]))
                            s.wait()
                            s.done(pool.tensor_tensor(pk[l][:, 2, :, :], ak[l][:, :, :], pk[l][:, 1, :, :], ALU.subtract))
                        elif name == "UNBIAS":
                            pool.wait_ge(tr_read, it * N_TR + o_done(l, 0))
                            s.wait_alone()
                            s.done(pool.memset(kc[l][PRODUCTS:BIAS, :, :], 0.0))
                    assert s.n == POOL_STEPS, s.n

            @block.vector
            def _(dve):
                with dve.Fori(0, TURNS) as it:
                    s = Steps(dve, dve_step, it, DVE_STEPS, dve_passed)
                    flat = lambda z: z[:, :, :].rearrange("p a b -> p (a b)")
                    wide = lambda z: z[:, :].unsqueeze(2).broadcast_to([P, NT, E])

                    def norm(l, src, dst):
                        for t in range(NT):
                            s.done(dve.bn_stats(stats[l][:, t, :], src[l][:, t, :]))
                        s.wait_alone()
                        for t in range(NT):
                            s.done(dve.bn_aggr(mv[l][:, t, :], stats[l][:, t, :]))
                        s.wait()
                        inverse_root(dve, s, mv[l][:, :, 1], rstd[l][:, :], root_v[:, :], root_w[:, :])
                        for t in range(NT):
                            last = dve.tensor_scalar(dst[l][:, t, :], src[l][:, t, :], mv[l][:, t, 0:1], rstd[l][:, t:t + 1],
                                                     ALU.subtract, ALU.mult)
                            if t < NT - 1:
                                s.done(last)
                        return last

                    def produced(step):
                        dve.wait_ge(pre_ready[step[1]], it * N_PRE + PRE_AT[step] + 1)

                    for step in STEPS:
                        name, l, u, k = step
                        bank = pre_ps[l]
                        if name == "LN":
                            if u == 0:
                                dve.wait_ge(x_loaded[l], it * 80 + 80)
                            else:
                                if u < 3:
                                    dve.wait_ge(tr_read, it * N_TR + o_done(l, u - 1))
                                if u == 2:
                                    s.wait()
                                    s.done(dve.tensor_tensor(flat(o[l]), flat(o[l]), flat(moe[l]), ALU.add))
                                    s.wait()
                                if u < 3:
                                    gate = (0, 2)[u - 1]
                                    s.done(dve.scalar_tensor_tensor(out=flat(xs[l]), in0=flat(o[l]), scalar=tanh_g[:, gate:gate + 1],
                                                                    in1=flat(xs[l]), op0=ALU.mult, op1=ALU.add))
                                s.wait()
                            norm(l, xs, xn).then_inc(xn_ready[l], 1)
                        elif name == "SPLIT":
                            dve.wait_ge(pre_read[l], it * N_PRE + pre_done(("XT" if u == 0 else "Q", l, u, 0)))
                            s.done(dve.tensor_copy(pq[l][:, 0, :, :], aq[l][:, :, :]))
                            s.wait()
                            s.done(dve.tensor_tensor(aq[l][:, :, :], aq[l][:, :, :], pq[l][:, 0, :, :], ALU.subtract))
                            s.wait()
                            s.done(dve.tensor_copy(pq[l][:, 1, :, :], aq[l][:, :, :]))
                            s.wait()
                            dve.tensor_tensor(pq[l][:, 2, :, :], aq[l][:, :, :], pq[l][:, 1, :, :], ALU.subtract).then_inc(q_split[l], 1)
                        elif name == "V" and u == 1:
                            produced(step)
                            dve.tensor_tensor(va[l][:, :, :, 0:HD], bank[:, :].rearrange("p (t h d) -> p t h d", t=NT, h=H),
                                              bv[:, :].rearrange("p (h d) -> p h d", h=H).unsqueeze(1).broadcast_to([P, NT, H, HD]),
                                              ALU.add).then_inc(pre_read[l], 1)
                        elif name == "S":
                            n = S_AT[step]
                            h, src = k
                            dve.wait_ge(s_ready, it * N_S + n + 1)
                            dst, w = (mx3[l][:, h, :], 3 * P) if u == 3 else (mx[l][:, h, src:src + 1], 2 * T) if u == 2 else (mx[l][:, h, :], 2 * T)
                            parts = dst.shape[-1]
                            dve.tensor_reduce(dst, s_ps[n % 2][:, 0:w].rearrange("p (a b) -> p a b", a=parts), AX.X, ALU.max).then_inc(s_read, 1)
                        elif name == "M":
                            srcs = 2 if u == 2 else 1
                            hs = slice(k * HG, (k + 1) * HG)
                            dve.wait_ge(s_read, it * N_S + S_AT[("S", l, u, (k * HG + HG - 1, srcs - 1))] + 3)
                            if u == 3:
                                s.done(dve.tensor_copy(mx[l][:, hs, 0], mx3[l][:, hs, 0]))
                                s.done(dve.tensor_tensor(mx[l][:, hs, 1], mx3[l][:, hs, 1], mx3[l][:, hs, 2], ALU.max))
                                s.wait()
                            m = mx[l][:, hs, :].rearrange("p h t -> p t h")
                            part = [mp[l][k][:, :, j, :] for j in range(3)]
                            s.done(dve.tensor_scalar(part[0], m, -1.0, None, ALU.mult))
                            s.wait()
                            s.done(dve.scalar_tensor_tensor(out=mr[:, :, :], in0=m, scalar=-1.0, in1=part[0], op0=ALU.mult, op1=ALU.subtract))
                            s.wait()
                            s.done(dve.tensor_copy(part[1], mr[:, :, :]))
                            s.wait()
                            dve.tensor_tensor(part[2], mr[:, :, :], part[1], ALU.subtract).then_inc(m_ready, 1)
                        elif name == "OT":
                            dve.wait_ge(tr_ready, it * N_TR + TR_AT[step] + 1)
                            heads = tr_ps[:, 0:T].rearrange("p (t j w) -> p t j w", t=NT, j=QH)
                            s.done(dve.reciprocal(rden[:, :, :], heads[:, :, :, HD]))
                            s.wait()
                            dve.tensor_tensor(o[l][:, :, k * QH * HD:(k + 1) * QH * HD].rearrange("p t (j d) -> p t j d", j=QH), heads[:, :, :, 0:HD],
                                              rden[:, :, :].unsqueeze(3).broadcast_to([P, NT, QH, HD]), ALU.mult).then_inc(tr_read, 1)
                        elif name == "GATE":
                            produced(step)
                            logits = bank[:, 0:NT * E].rearrange("p (t e) -> p t e", t=NT)
                            if u == 1:
                                last = dve.tensor_tensor(lg[l][:, :, :], logits, bg0[:, :].unsqueeze(1).broadcast_to([P, NT, E]), ALU.add)
                            else:
                                last = dve.tensor_copy(lg[l][:, :, :], logits)
                            last.then_inc(pre_read[l], 1)
                            dve.wait_ge(pre_read[l], it * N_PRE + pre_done(step))
                            s.done(dve.tensor_reduce(t1[0][l][:, :], lg[l][:, :, :], AX.X, ALU.max))
                            s.wait()
                            dve.tensor_tensor(lg[l][:, :, :], lg[l][:, :, :], wide(t1[0][l]), ALU.subtract).then_inc(lg_ready[l], 1)
                        elif name == "TOP":
                            dve.wait_ge(lg_exp[l], it * 2 + (u == 3) + 1)
                            s.done(dve.tensor_reduce(t1[0][l][:, :], pr[l][:, :, :], AX.X, ALU.add))
                            s.wait()
                            s.done(dve.reciprocal(t1[1][l][:, :], t1[0][l][:, :]))
                            s.wait()
                            s.done(dve.tensor_tensor(pr[l][:, :, :], pr[l][:, :, :], wide(t1[1][l]), ALU.mult))
                            s.wait()
                            for j in range(2):
                                left = pr[l] if j == 0 else t8[0][l]
                                hot = t8[1 + j][l]
                                s.done(dve.tensor_reduce(t1[j][l][:, :], left[:, :, :], AX.X, ALU.max))
                                s.wait()
                                s.done(dve.tensor_tensor(hot[:, :, :], left[:, :, :], wide(t1[j][l]), ALU.is_equal))
                                s.wait()
                                s.done(dve.tensor_tensor(hot[:, :, :], hot[:, :, :], first[:, :, :], ALU.mult))
                                s.wait()
                                s.done(dve.tensor_reduce(t1[2][l][:, :], hot[:, :, :], AX.X, ALU.max))
                                s.wait()
                                s.done(dve.tensor_tensor(hot[:, :, :], hot[:, :, :], wide(t1[2][l]), ALU.is_equal))
                                s.wait()
                                if j == 0:
                                    s.done(dve.scalar_tensor_tensor(out=flat(t8[0][l]), in0=flat(hot), scalar=-2.0, in1=flat(pr[l]),
                                                                    op0=ALU.mult, op1=ALU.add))
                                    s.wait()
                            s.done(dve.tensor_tensor(flat(t8[0][l]), flat(t8[1][l]), flat(t8[2][l]), ALU.add))
                            if u == 1:
                                s.wait()
                                last = dve.tensor_tensor(comb[l][:, :, :], pr[l][:, :, :], t8[0][l][:, :, :], ALU.mult)
                            else:
                                s.done(dve.tensor_tensor(t1[2][l][:, :], t1[0][l][:, :], t1[1][l][:, :], ALU.add))
                                s.wait()
                                s.done(dve.reciprocal(t1[3][l][:, :], t1[2][l][:, :]))
                                s.done(dve.tensor_tensor(pr[l][:, :, :], pr[l][:, :, :], t8[0][l][:, :, :], ALU.mult))
                                s.wait()
                                last = dve.tensor_tensor(comb[l][:, :, :], pr[l][:, :, :], wide(t1[3][l]), ALU.mult)
                            last.then_inc(top_done[l], 1)
                        elif name == "MBIAS":
                            produced(step)
                            dve.tensor_copy(flat(moe[l]), bank[:, :]).then_inc(pre_read[l], 1)
                        elif name == "EXPERT":
                            t, e = k
                            produced(step)
                            if e == 0:
                                dve.wait_ge(pre_read[l], it * N_PRE + pre_done(("MBIAS", l, u, 0)))
                                dve.wait_ge(top_done[l], it * 2 + 1)
                            for j in range(2):
                                s.wait()
                                last = dve.scalar_tensor_tensor(out=moe[l][:, t, :], in0=bank[:, j * D:(j + 1) * D], scalar=comb[l][:, t, e + j:e + j + 1],
                                                                in1=moe[l][:, t, :], op0=ALU.mult, op1=ALU.add)
                                if j == 0:
                                    s.done(last)
                            last.then_inc(pre_read[l], 1)
                            dve.wait_ge(pre_read[l], it * N_PRE + pre_done(step))
                        elif name == "PROJ":
                            produced(step)
                            if u == 2:
                                dve.scalar_tensor_tensor(out=flat(xs[l]), in0=bank[:, :], scalar=tanh_g[:, 1:2], in1=flat(xs[l]),
                                                         op0=ALU.mult, op1=ALU.add).then_inc(pre_read[l], 1)
                                dve.wait_ge(pre_read[l], it * N_PRE + pre_done(step))
                                s.done(dve.tensor_tensor(xs[l][:, :, :], xs[l][:, :, :], bproj[:, :].unsqueeze(1).broadcast_to([P, NT, D]), ALU.add))
                            else:
                                dve.tensor_tensor(flat(o[l]), bank[:, :], flat(xn[l]), ALU.add).then_inc(pre_read[l], 1)
                        elif name == "LNH":
                            dve.wait_ge(pre_read[l], it * N_PRE + pre_done(("PROJ", l, 3, 0)))
                            s.done(norm(l, o, moe))
                            s.wait()
                            s.done(dve.tensor_tensor(moe[l][:, :, :], moe[l][:, :, :], g1[:, :].unsqueeze(1).broadcast_to([P, NT, D]), ALU.mult))
                            s.wait()
                            dve.tensor_tensor(moe[l][:, :, :], moe[l][:, :, :], b1[:, :].unsqueeze(1).broadcast_to([P, NT, D]), ALU.add).then_inc(h_ready[l], 1)
                    assert s.n == DVE_STEPS, s.n


def expert_phase(nc, a):
    tanh_g, ident, out = a["tanh_g"], a["ident"], a["out"]
    own = ExitStack()
    with own:
        sb = lambda name, shape, dt=F32: own.enter_context(nc.sbuf_tensor(name, shape, dt))
        sem = lambda name: own.enter_context(nc.semaphore(name))
        lanes = range(LANES)
        lsb = lambda name, shape, dt=F32: [sb(f"{name}{l}", shape, dt) for l in lanes]
        lsem = lambda name: [sem(f"{name}{l}") for l in lanes]
        CH = E * FC
        GELUS = 4
        wup = sb("wup", [P, DC, E, F]); wdn = sb("wdn", [P, CH, D])
        bup = sb("bup", [P, CH]); bup_raw = sb("bup_raw", [CH, P]); bdn = sb("bdn", [E, D])
        g2 = sb("g2", [P, D]); b2 = sb("b2", [P, D])
        ht = lsb("ht", [P, DC, T]); x3 = lsb("x3", [P, NT, D]); hh = lsb("hh", [P, NT, D]); cw = lsb("cw", [P, NT, E])
        act_out = sb("act_out", [P, GELUS, T])
        acc = lsb("acc", [P, NT, D]); cwt = lsb("cwt", [E, T])
        stats = sb("stats2", [P, NT, 6]); mv = sb("mv2", [P, NT, 2]); rstd = sb("rstd2", [P, NT])
        root_v = sb("root_v2", [P, NT]); root_w = sb("root_w2", [P, NT])
        ps = lambda name: own.enter_context(nc.psum_tensor(name, [P, 512], F32))
        up_ps = [ps(f"up_ps{k}") for k in range(3)]
        dn_ps = [[ps(f"dn_ps{k}{t}") for t in range(NT)] for k in range(2)]
        mix_ps = ps("mix_ps")
        w_loaded, b_loaded, bup_turned, bup_ready = sem("ew_loaded"), sem("eb_loaded"), sem("bup_turned"), sem("bup_ready")
        loaded, mixed, mixed_read = lsem("loaded"), lsem("mixed"), lsem("mixed_read")
        up_ready, up_read, dn_ready, dn_read, finished, out_stored = sem("up_ready"), sem("up_read"), sem("dn_ready"), sem("dn_read"), lsem("finished"), lsem("out_stored")
        step, passed = sem("ffn_step"), sem("ffn_passed")
        N_UP, N_DN = LANES * CH, LANES * E

        with nc.Block() as block:
            @block.sync
            def _(sp):
                sp.dma_start(bup_raw[:, :], a["b_up"].rearrange("e (f p) -> (e f) p", p=P)).then_inc(b_loaded, 16)
                sp.dma_start(bdn[:, :], a["b_down"]).then_inc(b_loaded, 16)
                sp.dma_start(g2[:, :], a["ln2_g"].partition_broadcast(P)).then_inc(b_loaded, 16)
                sp.dma_start(b2[:, :], a["ln2_b"].partition_broadcast(P)).then_inc(b_loaded, 16)
                for e in range(E):
                    for c in range(DC):
                        sp.dma_start(wup[:, c, e, :], a["w_up"][e, c * P:(c + 1) * P, :]).then_inc(w_loaded, 16)
                    sp.dma_start(wdn[:, e * FC:(e + 1) * FC, :], a["w_down"][e].rearrange("(f p) n -> p f n", p=P)).then_inc(w_loaded, 16)
                for l in lanes:
                    sp.sem_inc(out_stored[l], 16)

            @block.tensor
            def _(pe):
                pe.wait_ge(b_loaded, 64)
                pe.transpose(mix_ps[:, 0:CH], bup_raw[:, :], ident[0:CH, 0:CH]).then_inc(bup_turned, 1)

            @block.vector
            def _(dve):
                dve.wait_ge(bup_turned, 1)
                dve.tensor_copy(bup[:, :], mix_ps[:, 0:CH]).then_inc(bup_ready, 1)
                dve.wait_ge(w_loaded, 16 * 3 * E)
                dve.sem_inc(dn_read, 2)

            @block.scalar
            def _(act):
                act.sem_inc(up_read, len(up_ps))

        with nc.Block() as block:
            @block.sync
            def _(sp):
                with sp.Fori(0, TURNS) as it:
                    batch = [sp.snap(it * LANES + l) for l in lanes]
                    for l in lanes:
                        one = lambda d: d[bass.ds(batch[l], 1)].rearrange("o p t n -> p (o t) n")
                        free = sp.snap(it * 16 + 16)
                        sp.wait_ge(out_stored[l], free)
                        for dst, src in ((ht, "ht_d"), (cw, "c_d"), (hh, "h_d"), (x3, "x3_d")):
                            sp.dma_start(dst[l][:, :, :], one(a[src])).then_inc(loaded[l], 16)
                    for l in lanes:
                        done = sp.snap(it + 1)
                        sp.wait_ge(finished[l], done)
                        sp.dma_start(out[bass.ds(batch[l], 1)].rearrange("o (t p) d -> p (o t) d", p=P), acc[l][:, :, :]).then_inc(out_stored[l], 16)
                for l in lanes:
                    sp.wait_ge(out_stored[l], 16 * (TURNS + 1))

            @block.tensor
            def _(pe):
                with pe.Fori(0, TURNS) as it:
                    def up(l, j):
                        n = l * CH + j
                        e, f = divmod(j, FC)
                        pe.wait_ge(up_read, it * N_UP + n + 1)
                        for c in range(DC):
                            last = pe.matmul(up_ps[n % len(up_ps)][:, 0:T], wup[:, c, e, f * P:(f + 1) * P], ht[l][:, c, :], start=c == 0, stop=c == DC - 1)
                        last.then_inc(up_ready, 1)

                    def down(l, j):
                        n = l * CH + j
                        e, f = divmod(j, FC)
                        m = l * E + e
                        pe.wait_ge(up_read, it * N_UP + n + 1 + len(up_ps))
                        if f == 0:
                            pe.wait_ge(dn_read, it * N_DN + m + 1)
                        for t in range(NT):
                            last = pe.matmul(dn_ps[m % 2][t][:, 0:D], act_out[:, n % GELUS, t * P:(t + 1) * P], wdn[:, j, :],
                                             start=f == 0, stop=f == FC - 1)
                        if f == FC - 1:
                            last.then_inc(dn_ready, 1)

                    for l in lanes:
                        pe.wait_ge(loaded[l], it * 64 + 64)
                        for t in range(NT):
                            last = pe.transpose(mix_ps[0:E, t * P:(t + 1) * P], cw[l][:, t, :], ident[:, :])
                        last.then_inc(mixed[l], 1)
                        pe.wait_ge(mixed_read[l], it * 2 + 1)
                        for t in range(NT):
                            last = pe.matmul(mix_ps[:, t * D:(t + 1) * D], cwt[l][:, t * P:(t + 1) * P], bdn[:, :], start=True, stop=True)
                        last.then_inc(mixed[l], 1)
                        up(l, 0)
                        up(l, 1)
                        for j in range(CH):
                            if j + 2 < CH:
                                up(l, j + 2)
                            down(l, j)
                        pe.wait_ge(mixed_read[l], it * 2 + 2)

            @block.scalar
            def _(act):
                with act.Fori(0, TURNS) as it:
                    for l in lanes:
                        for j in range(CH):
                            n = l * CH + j
                            act.wait_ge(up_ready, it * N_UP + n + 1)
                            act.activation(act_out[:, n % GELUS, :], up_ps[n % len(up_ps)][:, 0:T], ACT.Gelu_apprx_tanh,
                                           bias=bup[:, j:j + 1]).then_inc(up_read, 1)

            @block.vector
            def _(dve):
                with dve.Fori(0, TURNS) as it:
                    s = Steps(dve, step, it, FFN_STEPS, passed)
                    for l in lanes:
                        flat = lambda z: z[:, :, :].rearrange("p a b -> p (a b)")
                        dve.wait_ge(mixed[l], it * 2 + 1)
                        dve.tensor_copy(cwt[l][:, :], mix_ps[0:E, 0:T]).then_inc(mixed_read[l], 1)
                        dve.wait_ge(loaded[l], it * 64 + 64)
                        dve.wait_ge(mixed[l], it * 2 + 2)
                        dve.tensor_tensor(flat(acc[l]), mix_ps[:, :], flat(hh[l]), ALU.add).then_inc(mixed_read[l], 1)
                        dve.wait_ge(mixed_read[l], it * 2 + 2)
                        for e in range(E):
                            m = l * E + e
                            dve.wait_ge(dn_ready, it * N_DN + m + 1)
                            for t in range(NT):
                                last = dve.scalar_tensor_tensor(out=acc[l][:, t, :], in0=dn_ps[m % 2][t][:, 0:D], scalar=cw[l][:, t, e:e + 1],
                                                                in1=acc[l][:, t, :], op0=ALU.mult, op1=ALU.add)
                            last.then_inc(dn_read, 1)
                            dve.wait_ge(dn_read, it * N_DN + m + 3)
                        for t in range(NT):
                            s.done(dve.bn_stats(stats[:, t, :], acc[l][:, t, :]))
                        s.wait_alone()
                        for t in range(NT):
                            s.done(dve.bn_aggr(mv[:, t, :], stats[:, t, :]))
                        s.wait()
                        inverse_root(dve, s, mv[:, :, 1], rstd[:, :], root_v[:, :], root_w[:, :])
                        for t in range(NT):
                            s.done(dve.tensor_scalar(acc[l][:, t, :], acc[l][:, t, :], mv[:, t, 0:1], rstd[:, t:t + 1], ALU.subtract, ALU.mult))
                        s.wait()
                        row = lambda z: z[:, :].unsqueeze(1).broadcast_to([P, NT, D])
                        s.done(dve.tensor_tensor(acc[l][:, :, :], acc[l][:, :, :], row(g2), ALU.mult))
                        s.wait()
                        s.done(dve.tensor_tensor(acc[l][:, :, :], acc[l][:, :, :], row(b2), ALU.add))
                        s.wait()
                        dve.scalar_tensor_tensor(out=flat(acc[l]), in0=flat(acc[l]), scalar=tanh_g[:, 3:4], in1=flat(x3[l]),
                                                 op0=ALU.mult, op1=ALU.add).then_inc(finished[l], 1)
                    assert s.n == FFN_STEPS, s.n


_INS = ['x', 'ctx_2048', 'itok_Bx1_68_817', 'g_xattn', 'g_ffn', 'L0_xattn_b', 'L0_ffn_W_qkv', 'L0_ffn_b_qkv', 'L0_ffn_W_gate',
        'L0_ffn_b_gate', 'L0_ffn_W_experts', 'L0_ffn_b_experts', 'L1_xattn_w_qkv', 'L1_xattn_w_proj', 'L1_xattn_b_proj',
        'L1_ffn_w_qkv', 'L1_ffn_w_o', 'L1_ffn_g1', 'L1_ffn_b1', 'L1_ffn_wg', 'L1_ffn_w1', 'L1_ffn_bb1', 'L1_ffn_w2', 'L1_ffn_bb2',
        'L1_ffn_g2', 'L1_ffn_b2']


def kernel(**inputs):
    import numpy as _np
    import concourse.bacc as _bacc
    from concourse import mybir as _mybir
    from concourse.bass_utils import run_bass_kernel_spmd as _run

    nc = _bacc.Bacc("TRN2", target_bir_lowering=False, num_devices=1)
    arrays, args = {}, []
    for name in _INS:
        arr = _np.ascontiguousarray(inputs[name])
        arrays[f"in_{name}"] = arr
        args.append(nc.dram_tensor(f"in_{name}", arr.shape, _mybir.dt.from_np(arr.dtype), kind="ExternalInput").ap())
    args.append(nc.dram_tensor("out_0", [B, T, D], F32, kind="ExternalOutput").ap())
    build(nc, *args)
    r = _run(nc, [arrays], core_ids=[0])
    return r.results[0]["out_0"]
```

```python
from contextlib import ExitStack

import concourse.bass as bass
from concourse import mybir

F32 = mybir.dt.float32
BF16 = mybir.dt.bfloat16
I32 = mybir.dt.int32
U32 = mybir.dt.uint32
ALU = mybir.AluOpType
ACT = mybir.ActivationFunctionType
AX = mybir.AxisListType

P = 128
B, T, D = 16, 256, 256
H, HD, E = 16, 16, 8
F = 1024
NT = T // P
DC = D // P
FC = F // P
TILES = B * NT
TOPK = 2
SLOT_TILES = TILES * TOPK + E - 1
COLS = SLOT_TILES + 2
ROWS_OUT = B * T * TOPK
PAIRS, QT = B // 2, 2 * NT
RING = 4
LANES = 2
TURNS = B // LANES
G = 2
HG = H // G
QH = 4
VW = 32
SCALE = HD ** -0.5
EPS = 1e-5
MASKED = -1e12
FUTURE = -3e38
PRODUCTS = 6 * HD
BIAS = PRODUCTS + 3
ROWS = BIAS + 3
SINGLES = ((0, 1), (1, 2), (0, 2))
STACK_DMAS = 1 + len(SINGLES)
TWO_ONES = 1.0 + 0x3F80 * 2.0 ** -23
EXPS = 10
UNITS = ("l0 cross", "l0 self", "l1 joint", "l1 causal")


USES = {"LOAD": [("sp", 3.2), ("wire", 2.0)], "XT": [("pe", 0.7), ("act", 0.5)], "KT": [("pe", 0.7), ("act", 1.0)],
        "K": [("pe", 2.2), ("act", 1.0)], "Q": [("pe", 1.8), ("act", 1.0)], "V": [("pe", 1.8), ("act", 0.5)],
        "KSPLIT": [("pool", 4.3)], "QSPLIT": [("dve", 1.8)], "STACKW": [("sp", 0.9), ("wire", 2.2)], "STACKR": [("sp", 3.8), ("wire", 2.0)],
        "UNBIAS": [("pool", 3.5)], "GATE": [("pe", 0.8), ("dve", 0.5)], "GEXP": [("act", 0.1)], "TOP": [("dve", 0.5)],
        "CT": [("pe", 0.2), ("act", 0.3)], "MBIAS": [("pe", 0.9), ("dve", 0.6)], "EXPERT": [("pe", 1.8), ("dve", 0.9)],
        "S": [("pe", 0.28), ("dve", 0.6)], "M": [("dve", 0.7)], "MT": [("pe", 0.15), ("act", 0.26), ("sp", 1.4), ("wire", 2.0)],
        "T": [("pe", 0.28), ("act", 0.48)], "PV": [("pe", 1.1), ("act", 0.26)], "OT": [("pe", 0.25), ("dve", 0.44)],
        "OTT": [("pe", 0.5), ("act", 0.5)], "PROJ": [("pe", 2.0), ("dve", 0.6)], "STORE": [("sp", 0.9), ("wire", 2.0)]}
USES_OF_UNIT = {("XT", 0): [("pe", 0.7), ("act", 1.0)], ("K", 1): [("pe", 2.2), ("act", 1.4)], ("Q", 1): [("pe", 1.8), ("act", 1.4)],
                ("V", 1): [("pe", 1.8), ("dve", 0.6)], ("S", 3): [("pe", 0.33), ("dve", 0.47)], ("T", 3): [("pe", 0.33), ("act", 0.37)],
                ("M", 3): [("dve", 1.0)], ("PV", 2): [("pe", 2.1), ("act", 0.26)], ("PROJ", 2): [("pe", 2.0), ("dve", 1.4)]}
LN_US = (1.0, 1.8, 2.6, 1.0)
HOP_US = 0.17
LATER_US = {"UNBIAS": -45.1, "TOP": -104.5, "QSPLIT": -1.4, "V": 0.4, "M": -1.6, "MBIAS": 0.4, "STACKR": -17.5, "STORE": -8.9,
            "Q": -13.0, "STACKW": 1.1, "LN": -1.8, "KSPLIT": 0.2, "OTT": 0.3, "PROJ": -0.3, "EXPERT": 0.1, "K": 0.3, "XT": 0.2,
            "OT": -0.2}
LONG_WAY = 0.002
LAG_US = 4
NEWTON = 3
SUBSTEPS = {"LN": 3 + NEWTON, "TOP": 6}
AHEAD = ("LOAD", "LN", "XT", "KT", "KSPLIT", "QSPLIT", "STACKW", "STACKR")
PRE = ("XT", "KT", "Q", "K", "V", "GATE", "CT", "MBIAS", "EXPERT", "OTT", "PROJ")


def is_ahead(step):
    return step[0] in AHEAD and step[1:3] == (0, 0)


def lane_threads(l):
    operands, projected, scores, maxima, exps, outputs, side, needs = [], [], [], [], [], [], [], {}

    def add(to, name, u, k, *on):
        step = (name, l, u, k)
        to.append(step)
        needs[step] = [x for x in on if x]
        return step

    done = None
    for u in range(4):
        srcs = 2 if u == 2 else 1
        ready = add(operands, "LOAD", u, 0) if u == 0 else done
        keys = add(operands, "KT", u, 0, ready) if u == 0 else None
        if u == 0:
            key_parts = add(operands, "KSPLIT", u, 0, keys)
        for k in range(SUBSTEPS["LN"]):
            ready = add(operands, "LN", u, k, ready, expert if u == 2 else None)
        turned = queries = add(operands, "XT", u, 0, ready)
        values = keys
        if u:
            keys = add(operands, "K", u, 0, turned)
            key_parts = add(operands, "KSPLIT", u, 0, keys)
            queries = add(operands, "Q", u, 0, turned)
        query_parts = add(operands, "QSPLIT", u, 0, queries)
        written = add(operands, "STACKW", u, 0, key_parts, query_parts)
        if u:
            values = add(projected, "V", u, 0, turned)
        if u == 1:
            chain = add(side, "GEXP", u, 0, add(side, "GATE", u, 0, turned))
            add(side, "UNBIAS", u, 0, done)
            for k in range(SUBSTEPS["TOP"]):
                chain = add(side, "TOP", u, k, chain)
            chain = add(side, "MBIAS", u, 0, add(side, "CT", u, 0, chain))
            for t in range(NT):
                for e in range(0, E, 2):
                    expert = add(side, "EXPERT", u, (t, e), chain)
        rows = add(operands, "STACKR", u, 0, written)
        slots = [(h, s) for h in range(H) for s in range(srcs)]
        for g in range(G):
            mine = [add(scores, "S", u, x, rows) for x in slots if x[0] // HG == g]
            split = add(maxima, "MT", u, g, add(maxima, "M", u, g, *mine))
            for q in range(g * HG // QH, (g + 1) * HG // QH):
                parts = [add(exps, "T", u, x, split) for x in slots if x[0] // QH == q]
                done = add(outputs, "OT", u, q, add(outputs, "PV", u, q, values, *parts))
        if u >= 2:
            done = add(outputs, "PROJ", u, 0, add(outputs, "OTT", u, 0, done))
    add(outputs, "STORE", 3, 0, done)
    return [outputs, exps, maxima, scores, operands, side, projected], needs


def merged_steps():
    threads, needs = [], {}
    for l in range(LANES):
        mine, on = lane_threads(l)
        needs.update(on)
        if l == 0:
            ahead = [s for s in needs if is_ahead(s)]
            for s in needs:
                needs[s] = [x for x in needs[s] if is_ahead(s) or not is_ahead(x)]
            needs[ahead[0]] = [("STORE", 0, 3, 0)]
            mine = [[s for s in thread if not is_ahead(s)] for thread in mine] + [ahead]
        threads += mine
    order, end, free, banks, tail = [], {}, {}, {}, {}
    users = {}
    for step, on in needs.items():
        for x in on:
            users.setdefault(x, []).append(step)

    def tail_of(step):
        if step not in tail:
            tail[step] = sum(us + HOP_US for _, us in uses_of(step)) + max([tail_of(x) for x in users.get(step, [])], default=0)
        return tail[step]

    while any(threads):
        best = None
        for thread in threads:
            if not thread or any(x not in end for x in needs[thread[0]]):
                continue
            step = thread[0]
            name, l, u, k = step
            bank = name if name in "ST" else "tr" if name in ("MT", "OT") else "pv" if name == "PV" else l if name in PRE else None
            slots = 2 if name in ("S", "T") else 1
            used = banks.get(bank, [])
            if name == "T" and len(banks.get(("ex", l), [])) >= EXPS and banks[("ex", l)][-EXPS] not in end:
                continue
            if name == "PV" and len(banks.get("ot", [])) >= 2 and banks["ot"][-2] not in end:
                continue
            start = max([l * LAG_US] + [end[x] + HOP_US for x in needs[step]])
            if bank is not None and len(used) >= slots:
                start = max(start, used[-slots] + HOP_US)
            start = max(start, free.get(uses_of(step)[0][0], 0))
            score = start + LATER_US.get(name, 0) - LONG_WAY * tail_of(step)
            if best is None or score < best[0]:
                best = (score, start, thread, bank)
        _, now, thread, bank = best
        step = thread.pop(0)
        name, l, u, k = step
        for engine, us in uses_of(step):
            if engine != "wire":
                now = max(now, free.get(engine, 0))
            now += us
            if engine != "wire":
                free[engine] = now
            now += HOP_US
        end[step] = now - HOP_US
        if bank is not None:
            banks.setdefault(bank, []).append(end[step])
        if name == "T":
            banks.setdefault(("ex", l), []).append(("PV", l, u, k[0] // QH))
        if name == "PV":
            banks.setdefault("ot", []).append(("OT", l, u, k))
        order.append(step)
    return order


def uses_of(step):
    name, l, u, k = step
    if name == "LN":
        return [("dve", LN_US[u] if k == 0 else 0.65 if k == SUBSTEPS["LN"] - 1 else 0.47)]
    return USES_OF_UNIT.get((name, u), USES.get(name))


def turn_of(step, turn):
    return turn + 1 if is_ahead(step) else turn


STEPS = merged_steps()
HEAD = [s for s in STEPS if is_ahead(s)]

def numbered(keys):
    return {k: n for n, k in enumerate(keys)}


S_AT = numbered(s for s in STEPS if s[0] == "S")
T_AT = numbered(s for s in STEPS if s[0] == "T")
EX_AT = {}
for _l in range(LANES):
    EX_AT.update(numbered(s for s in STEPS if s[0] == "T" and s[1] == _l))
M_AT = numbered(s for s in STEPS if s[0] == "M")
PV_AT = numbered(s for s in STEPS if s[0] == "PV")
TR_AT = numbered(s for s in STEPS if s[0] in ("MT", "OT"))
PRE_AT = {}
for _l in range(LANES):
    PRE_AT.update(numbered(s for s in sorted(STEPS, key=lambda s: not is_ahead(s)) if s[0] in PRE and s[1] == _l))
N_S, N_T, N_M, N_PV, N_TR = len(S_AT), len(T_AT), len(M_AT), len(PV_AT), len(TR_AT)
N_PRE = len(PRE_AT) // LANES
class Steps:

    def __init__(self, eng, sem, turn=0, per_turn=0, passed=None, before=0):
        self.eng, self.sem, self.base, self.n, self.passed = eng, sem, turn * per_turn + before, 0, passed

    def done(self, ins):
        ins.then_inc(self.sem, 1)
        self.n += 1

    def wait(self):
        self.eng.wait_ge(self.sem, self.base + self.n)

    def wait_alone(self):
        self.wait()
        self.stand()

    def stand(self):
        self.eng.sem_inc(self.passed, 1)


RSQRT_GUESS = 0x5F3759DF
DVE_STEPS, DVE_HEAD = 296, 19
POOL_STEPS, POOL_HEAD = 28, 4
ROUTE_STEPS, COMBINE_STEPS = 84, 120


def root_guess(dve, s, var, out, v):
    s.done(dve.tensor_scalar(v, var, EPS, None, ALU.add))
    s.wait()
    s.done(dve.tensor_scalar(out.bitcast(I32), v.bitcast(I32), 1, None, ALU.logical_shift_right))
    s.wait()
    s.done(dve.tensor_scalar(out.bitcast(I32), out.bitcast(I32), -1.0, float(RSQRT_GUESS), ALU.mult, ALU.add))


def root_step(dve, s, out, v, w):
    s.done(dve.tensor_tensor(w, out, out, ALU.mult))
    s.wait()
    s.done(dve.scalar_tensor_tensor(out=w, in0=w, scalar=-0.5, in1=v, op0=ALU.mult, op1=ALU.mult))
    s.wait()
    s.done(dve.scalar_tensor_tensor(out=out, in0=w, scalar=1.5, in1=out, op0=ALU.add, op1=ALU.mult))


def inverse_root(dve, s, var, out, v, w):
    root_guess(dve, s, var, out, v)
    s.wait()
    for _ in range(NEWTON):
        root_step(dve, s, out, v, w)
        s.wait()


def norm_moments(dve, s, src, stats, mv, rstd, root_v, root_w, n):
    for t in range(n):
        s.done(dve.bn_stats(stats[:, t, :], src[:, t, :]))
    s.wait_alone()
    for t in range(n):
        s.done(dve.bn_aggr(mv[:, t, :], stats[:, t, :]))
    s.wait()
    inverse_root(dve, s, mv[:, :, 1], rstd[:, :], root_v[:, :], root_w[:, :])


def build(nc, x, ctx_in, itok, g_xattn, g_ffn, key_b, w0_qkv, b0_qkv, w0_gate, b0_gate, w0_exp, b0_exp,
          w1x_qkv, w1x_proj, b1x_proj, w1_qkv, w1_o, ln1_g, ln1_b, w1_gate, w_up, b_up, w_down, b_down,
          ln2_g, ln2_b, out):
    dram = lambda name, shape, dt: nc.dram_tensor(name, shape, dt, kind="Internal").ap()
    bias_d = dram("key_bias_parts", [B, 3, T], BF16)
    q_d = [dram(f"q_parts_{l}", [H, HD, 3, T], BF16) for l in range(LANES)]
    k_d = [dram(f"k_parts_{l}", [H, HD, 3, T], BF16) for l in range(LANES)]
    x3_d = dram("x3", [B, P, NT, D], F32)
    h_d = dram("h", [B, P, NT, D], F32)
    hn_d = dram("h_normed", [B, P, NT, D], F32)
    y_d = dram("expert_rows", [B, P, NT * TOPK, D], F32)
    keep = ExitStack()
    with keep:
        tanh_g = keep.enter_context(nc.sbuf_tensor("tanh_g", [P, 4], F32))
        ident = keep.enter_context(nc.sbuf_tensor("ident", [P, P], F32))
        attention_phase(nc, locals())
        expert_phase(nc, locals())


def attention_phase(nc, a):
    x, ctx_in, tanh_g, ident = a["x"], a["ctx_in"], a["tanh_g"], a["ident"]
    bias_d, q_d, k_d = a["bias_d"], a["q_d"], a["k_d"]
    own = ExitStack()
    with own:
        sb = lambda name, shape, dt=F32: own.enter_context(nc.sbuf_tensor(name, shape, dt))
        sem = lambda name: own.enter_context(nc.semaphore(name))
        lanes = range(LANES)
        lsb = lambda name, shape, dt=F32: [sb(f"{name}{l}", shape, dt) for l in lanes]
        lsem = lambda name: [sem(f"{name}{l}") for l in lanes]
        w0 = sb("w0", [P, DC, 3 * D]); w1x = sb("w1x", [P, DC, 3 * D]); w1 = sb("w1", [P, DC, 3 * D])
        wproj = sb("wproj", [P, DC, D]); wo = sb("wo", [P, DC, D])
        wexp = sb("wexp", [P, DC, E, D]); bexp = sb("bexp", [E, D])
        wg0 = sb("wg0", [P, DC, E]); bg0 = sb("bg0", [P, E])
        bqk = sb("bqk", [P, 4]); bv = sb("bv", [P, D]); bproj = sb("bproj", [P, D])
        ident_b = sb("ident_b", [P, P], BF16)
        late_k = sb("late_k", [P, P], BF16)
        late_q = sb("late_q", [P, P], BF16)
        first = sb("first", [P, NT, E])
        xs = lsb("xs", [P, NT, D]); ctx = lsb("ctx", [P, NT, 2 * D])
        xn = lsb("xn", [P, NT, D]); xt = lsb("xt", [P, DC, T])
        aq = lsb("aq", [P, DC, T]); ak = lsb("ak", [P, DC, T])
        pq = lsb("pq", [P, DC, 3, T], BF16); pk = lsb("pk", [P, DC, 3, T], BF16)
        qs = lsb("qs", [ROWS, H, T], BF16); ks = lsb("ks", [ROWS, H, T], BF16); kc = lsb("kc", [ROWS, H, T], BF16)
        va = lsb("va", [P, NT, H, VW]); vc = lsb("vc", [P, NT, H, VW])
        mx = lsb("mx", [P, H, 2]); mx3 = lsb("mx3", [P, H, 3])
        mr = sb("mr", [P, NT, HG]); mp = [[sb(f"mp{l}{g}", [P, NT, 3, HG], BF16) for g in range(G)] for l in lanes]
        mt = [[sb(f"mt{l}{g}", [3 * HG, T], BF16) for g in range(G)] for l in lanes]
        ex = lsb("ex", [P, EXPS, 2 * T])
        ot = [sb(f"ot{k}", [P, T]) for k in range(2)]
        rden = sb("rden", [P, NT, QH])
        o = lsb("o", [P, NT, D]); moe = lsb("moe", [P, NT, D])
        stats = lsb("stats", [P, NT, 6]); mv = lsb("mv", [P, NT, 2]); rstd = lsb("rstd", [P, NT])
        root_v = lsb("root_v", [P, NT]); root_w = lsb("root_w", [P, NT])
        lg = lsb("lg", [P, NT, E]); pr = lsb("pr", [P, NT, E]); comb = lsb("comb", [P, NT, E])
        t8 = [lsb(f"t8_{k}_", [P, NT, E]) for k in range(3)]
        t1 = [lsb(f"t1_{k}_", [P, NT]) for k in range(4)]
        combt = lsb("combt", [E, T])
        lens = sb("lens", [B, 1], I32); lenf = sb("lenf", [B, 1])
        keyi = xs[0][0:B, 0, :].bitcast(I32); kbf = xs[0][0:B, 1, :]; kbb = xs[1][0:B, 0, :]; kbp = pq[0][0:B, 0, :, :]

        ps = lambda name: own.enter_context(nc.psum_tensor(name, [P, 512], F32))
        s_ps = [ps(f"s_ps{k}") for k in range(2)]
        t_ps = [ps(f"t_ps{k}") for k in range(2)]
        pv_ps = ps("pv_ps")
        tr_ps = ps("tr_ps")
        pre_ps = [ps(f"pre_ps{l}") for l in lanes]
        tr_b = tr_ps[:, :].bitcast(BF16)

        w_loaded, small_loaded, raw_loaded, itok_loaded = sem("w_loaded"), sem("small_loaded"), sem("raw_loaded"), sem("itok_loaded")
        consts_ready, setup_step, bias_ready, bias_stored = sem("consts_ready"), sem("setup_step"), sem("bias_ready"), sem("bias_stored")
        raw_turned, raw_copied, tanh_ready, pool_setup = sem("raw_turned"), sem("raw_copied"), sem("tanh_ready"), sem("pool_setup")
        x_loaded, xn_ready, vc_ready, unbiased = lsem("x_loaded"), lsem("xn_ready"), lsem("vc_ready"), lsem("unbiased")
        pre_ready, pre_read = lsem("pre_ready"), lsem("pre_read")
        q_split, k_split, q_stored, k_stored = lsem("q_split"), lsem("k_split"), lsem("q_stored"), lsem("k_stored")
        q_rows, k_rows = lsem("q_rows"), lsem("k_rows")
        max_rows = [[sem(f"max_rows{l}{g}") for g in range(G)] for l in lanes]
        s_ready, s_read, t_ready, t_read = sem("s_ready"), sem("s_read"), sem("t_ready"), sem("t_read")
        m_ready, tr_ready, tr_read, pv_ready, pv_read = sem("m_ready"), sem("tr_ready"), sem("tr_read"), sem("pv_ready"), sem("pv_read")
        lg_ready, lg_exp, top_done, h_ready, stored = lsem("lg_ready"), lsem("lg_exp"), lsem("top_done"), lsem("h_ready"), lsem("stored")
        dve_step, pool_done, dve_passed, pool_passed = sem("dve_step"), sem("pool_done"), sem("dve_passed"), sem("pool_passed")

        W_DMAS, SMALL_DMAS, RAW_DMAS, STORES = 5, 8, 2, 2
        raw = ex[0][:, :, :].rearrange("p a b -> p (a b)")[:, 0:8 * D].rearrange("p (r n) -> p r n", n=D)

        with nc.Block() as block:
            @block.sync
            def _(sp):
                sp.dma_start(lens[:, :], a["itok"]).then_inc(itok_loaded, 16)
                sp.dma_start(kbb[:, :], a["key_b"].partition_broadcast(B)).then_inc(itok_loaded, 16)
                sp.dma_start(raw[:, 0:6, :], a["w1x_qkv"].rearrange("(r p) n -> p r n", p=P)).then_inc(raw_loaded, 16)
                sp.dma_start(raw[:, 6:8, :], a["w1x_proj"].rearrange("(r p) n -> p r n", p=P)).then_inc(raw_loaded, 16)
                sp.dma_start(tanh_g[:, 0:2], a["g_xattn"].partition_broadcast(P)).then_inc(small_loaded, 16)
                sp.dma_start(tanh_g[:, 2:4], a["g_ffn"].partition_broadcast(P)).then_inc(small_loaded, 16)
                sp.dma_start(bqk[:, :], a["b0_qkv"][0:2 * D].rearrange("(c p) -> p c", p=P), allow_slow_non_contiguous=True).then_inc(small_loaded, 16)
                sp.dma_start(bv[:, :], a["b0_qkv"][2 * D:3 * D].partition_broadcast(P)).then_inc(small_loaded, 16)
                sp.dma_start(bg0[:, :], a["b0_gate"].partition_broadcast(P)).then_inc(small_loaded, 16)
                sp.dma_start(bproj[:, :], a["b1x_proj"].partition_broadcast(P)).then_inc(small_loaded, 16)
                sp.dma_start(bexp[:, :], a["b0_exp"]).then_inc(small_loaded, 16)
                sp.dma_start(wg0[:, :, :], a["w0_gate"].rearrange("(c p) n -> p c n", p=P)).then_inc(small_loaded, 16)
                chunked = lambda w: w.rearrange("(c p) n -> p c n", p=P)
                sp.dma_start(w0[:, :, :], chunked(a["w0_qkv"])).then_inc(w_loaded, 16)
                for c in range(DC):
                    sp.dma_start(wexp[:, c, :, :], a["w0_exp"][:, c * P:(c + 1) * P, :].rearrange("e p n -> p e n")).then_inc(w_loaded, 16)
                sp.dma_start(w1[:, :, :], chunked(a["w1_qkv"])).then_inc(w_loaded, 16)
                sp.dma_start(wo[:, :, :], chunked(a["w1_o"])).then_inc(w_loaded, 16)
                sp.wait_ge(bias_ready, 1)
                sp.dma_start(bias_d, kbp[:, :, :]).then_inc(bias_stored, 16)
                sp.wait_ge(bias_stored, 16)
                sp.wait_ge(w_loaded, 16 * W_DMAS)
                for l in lanes:
                    sp.sem_inc(stored[l], 16 * STORES)

            @block.gpsimd
            def _(pool):
                pool.memset(ident[:, :], 0.0).then_inc(pool_setup, 1)
                pool.memset(late_k[:, :], 0.0).then_inc(pool_setup, 1)
                pool.memset(late_q[:, :], 0.0).then_inc(pool_setup, 1)
                pool.wait_ge(pool_setup, 3)
                pool.affine_select(out=ident[:, :], in_=ident[:, :], compare_op=ALU.not_equal, fill=1.0, base=0,
                                   pattern=[[-1, P]], channel_multiplier=1).then_inc(pool_setup, 1)
                pool.affine_select(out=late_k[:, :], in_=late_k[:, :], compare_op=ALU.is_ge, fill=FUTURE, base=0,
                                   pattern=[[-1, P]], channel_multiplier=1).then_inc(pool_setup, 1)
                pool.affine_select(out=late_q[:, :], in_=late_q[:, :], compare_op=ALU.is_ge, fill=FUTURE, base=0,
                                   pattern=[[1, P]], channel_multiplier=-1).then_inc(pool_setup, 1)
                pool.iota(keyi[:, :], pattern=[[1, T]], base=0, channel_multiplier=0).then_inc(pool_setup, 1)
                pool.wait_ge(pool_setup, 4)
                pool.tensor_copy(ident_b[:, :], ident[:, :]).then_inc(consts_ready, 1)
                for l in lanes:
                    for v in (va[l], vc[l]):
                        pool.memset(v[:, :, :, :], 0.0).then_inc(pool_setup, 1)
                pool.wait_ge(pool_setup, 7 + 2 * LANES)
                pool.sem_inc(pool_done, 1)
                for l in lanes:
                    for v in (va[l], vc[l]):
                        pool.memset(v[:, :, :, HD:HD + 1], 1.0).then_inc(consts_ready, 1)

            @block.vector
            def _(dve):
                s = Steps(dve, setup_step)
                dve.wait_ge(itok_loaded, 32)
                dve.wait_ge(pool_setup, 7)
                s.done(dve.tensor_copy(lenf[:, :], lens[:, :]))
                s.done(dve.tensor_copy(kbf[:, :], keyi[:, :]))
                s.wait()
                s.done(dve.tensor_scalar(kbf[:, :], kbf[:, :], lenf[:, 0:1], 1.0, ALU.is_lt, ALU.subtract))
                s.wait()
                s.done(dve.scalar_tensor_tensor(out=kbf[:, :], in0=kbf[:, :], scalar=-MASKED, in1=kbb[:, :], op0=ALU.mult, op1=ALU.add))
                s.wait()
                s.done(dve.tensor_copy(kbp[:, 0, :], kbf[:, :]))
                s.wait()
                s.done(dve.tensor_tensor(kbf[:, :], kbf[:, :], kbp[:, 0, :], ALU.subtract))
                s.wait()
                s.done(dve.tensor_copy(kbp[:, 1, :], kbf[:, :]))
                s.wait()
                dve.tensor_tensor(kbp[:, 2, :], kbf[:, :], kbp[:, 1, :], ALU.subtract).then_inc(bias_ready, 1)
                for l in lanes:
                    for z in (qs[l], ks[l], kc[l]):
                        s.done(dve.memset(z[PRODUCTS:ROWS, :, :].bitcast(F32), TWO_ONES))
                for k in range(E):
                    s.done(dve.memset(first[:, :, k:k + 1], float(E - k)))
                s.wait()
                for l in lanes:
                    s.done(dve.memset(ks[l][PRODUCTS:BIAS, :, :].bitcast(F32), 0.0))
                dve.wait_ge(small_loaded, 16 * SMALL_DMAS)
                s.done(dve.tensor_scalar(bqk[:, 0:2], bqk[:, 0:2], SCALE, None, ALU.mult))
                dve.wait_ge(tanh_ready, 1)
                s.done(dve.tensor_scalar(bproj[:, :], bproj[:, :], tanh_g[:, 1:2], None, ALU.mult))
                for k in range(8):
                    dve.wait_ge(raw_turned, k + 1)
                    dst = w1x[:, :, k * P:(k + 1) * P] if k < 6 else wproj[:, :, (k - 6) * P:(k - 5) * P]
                    dve.tensor_copy(dst, s_ps[k % 2][:, 0:D].rearrange("p (c n) -> p c n", c=DC)).then_inc(raw_copied, 1)
                s.wait()
                dve.sem_inc(s_read, 2)
                dve.sem_inc(tr_read, 1)
                for l in lanes:
                    dve.sem_inc(pre_read[l], 1)

            @block.scalar
            def _(act):
                act.wait_ge(small_loaded, 16 * SMALL_DMAS)
                act.activation(tanh_g[:, :], tanh_g[:, :], ACT.Tanh).then_inc(tanh_ready, 1)
                act.sem_inc(t_read, 2)
                act.sem_inc(pv_read, 1)

            @block.tensor
            def _(pe):
                pe.wait_ge(raw_loaded, 16 * RAW_DMAS)
                pe.wait_ge(pool_setup, 4)
                for k in range(8):
                    if k >= 2:
                        pe.wait_ge(raw_copied, k - 1)
                    for c in range(DC):
                        last = pe.transpose(s_ps[k % 2][:, c * P:(c + 1) * P], raw[:, k, c * P:(c + 1) * P], ident[:, :])
                    last.then_inc(raw_turned, 1)

        def o_done(l, u):
            return TR_AT[("OT", l, u, H // QH - 1)] + 2

        def pre_done(step):
            return PRE_AT[step] + 2

        with nc.Block() as block:
            @block.sync
            def _(sp):
                def stages(steps, turn):
                    def wait_all(*pairs):
                        values = [v if isinstance(v, int) else sp.snap(v) for _, v in pairs]
                        for (s, _), v in zip(pairs, values):
                            sp.wait_ge(s, v)

                    for step in steps:
                        it = turn_of(step, turn)
                        name, l, u, k = step
                        if name == "LOAD":
                            one = lambda d: d[bass.ds(it + l * TURNS, 1)]
                            wait_all((stored[l], it * 16 * STORES + 16 * STORES))
                            sp.dma_start(xs[l][:, :, :], one(x).rearrange("o (t p) d -> p (o t) d", p=P)).then_inc(x_loaded[l], 16)
                            sp.dma_start(ctx[l][:, :, :], one(ctx_in).rearrange("o (t p) d -> p (o t) d", p=P)).then_inc(x_loaded[l], 16)
                            for part in range(3):
                                row = one(bias_d)[:, part, :].unsqueeze(1).broadcast_to([1, H, T])
                                sp.dma_start(kc[l][PRODUCTS + part:PRODUCTS + part + 1, :, :], row).then_inc(x_loaded[l], 16)
                        if name == "STACKW":
                            for parts, ready, value, dst, done in ((pk[l], k_split[l], it * 4 + u + 1, k_d[l], k_stored[l]),
                                                                   (pq[l], q_split[l], it * 4 + u + 1, q_d[l], q_stored[l])):
                                wait_all((ready, value))
                                sp.dma_start(dst.rearrange("(c h) d a t -> (h d) c (a t)", c=DC),
                                             parts[:, :, :, :].rearrange("p c a t -> p c (a t)")).then_inc(done, 16)
                        if name == "STACKR":
                            kst = kc if u == 0 else ks
                            for operand, src, stored_, dst, done in ((0, q_d[l], q_stored[l], qs[l], q_rows[l]),
                                                                     (1, k_d[l], k_stored[l], kst[l], k_rows[l])):
                                wait_all((stored_, it * 4 * 16 + (u + 1) * 16))
                                sp.dma_start(dst[0:3 * HD, :, :], src.rearrange("h d a t -> (d a) h t")).then_inc(done, 16)
                                for r, parts in enumerate(SINGLES):
                                    sp.dma_start(dst[(3 + r) * HD:(4 + r) * HD, :, :],
                                                 src[:, :, parts[operand], :].rearrange("h d t -> d h t")).then_inc(done, 16)
                        if name == "MT":
                            r = TR_AT[(name, l, u, k)]
                            wait_all((tr_read, it * N_TR + r + 2))
                            for part in range(3):
                                sp.dma_start(qs[l][BIAS + part:BIAS + part + 1, k * HG:(k + 1) * HG, :],
                                             mt[l][k][part * HG:(part + 1) * HG, :]).then_inc(max_rows[l][k], 16)
                        if name == "STORE":
                            one = lambda d: d[bass.ds(it + l * TURNS, 1)].rearrange("o p t n -> p (o t) n")
                            wait_all((pre_read[l], it * N_PRE + pre_done(("PROJ", l, 3, 0))))
                            sp.dma_start(one(a["x3_d"]), xs[l][:, :, :]).then_inc(stored[l], 16)
                            sp.dma_start(one(a["h_d"]), o[l][:, :, :]).then_inc(stored[l], 16)

                stages(HEAD, -1)
                with sp.Fori(0, TURNS) as turn:
                    stages(STEPS, turn)
                for l in lanes:
                    sp.wait_ge(stored[l], 16 * STORES * (TURNS + 1))
                sp.wait_ge(x_loaded[0], 80 * (TURNS + 1))
                sp.wait_ge(q_rows[0], (TURNS * 4 + 1) * 16 * STACK_DMAS)
                sp.wait_ge(k_rows[0], (TURNS * 4 + 1) * 16 * STACK_DMAS)

            @block.tensor
            def _(pe):
                nc.disable_value_cache = True
                def stages(steps, turn):
                    def begin_pre(step):
                        pe.wait_ge(pre_read[step[1]], it * N_PRE + PRE_AT[step] + 1)

                    def turn_tokens(dst, src):
                        for c in range(DC):
                            for t in range(NT):
                                last = pe.transpose(dst[:, c * T + t * P:c * T + (t + 1) * P], src[:, t, c * P:(c + 1) * P], ident[:, :])
                        return last

                    def project_t(dst, w, at, src):
                        for half in range(DC):
                            for c in range(DC):
                                last = pe.matmul(dst[:, half * T:(half + 1) * T], w[:, c, at + half * P:at + (half + 1) * P],
                                                 src[:, c, :], start=c == 0, stop=c == DC - 1)
                        return last

                    def project(dst, w, src, n):
                        for t in range(NT):
                            for c in range(DC):
                                last = pe.matmul(dst[:, t * n:(t + 1) * n], src[:, c, t * P:(t + 1) * P], w[:, c, :],
                                                 start=c == 0, stop=c == DC - 1)
                        return last

                    for step in steps:
                        it = turn_of(step, turn)
                        name, l, u, k = step
                        bank = pre_ps[l]
                        w_of = (None, w0, w1x, w1)[u]
                        if name == "XT":
                            pe.wait_ge(xn_ready[l], it * 4 + u + 1)
                            begin_pre(step)
                            turn_tokens(bank, xn[l]).then_inc(pre_ready[l], 1)
                        elif name == "KT":
                            pe.wait_ge(x_loaded[l], it * 80 + 80)
                            begin_pre(step)
                            turn_tokens(bank, ctx[l]).then_inc(pre_ready[l], 1)
                        elif name in ("Q", "K"):
                            begin_pre(step)
                            project_t(bank, w_of, 0 if name == "Q" else D, xt[l]).then_inc(pre_ready[l], 1)
                        elif name == "V":
                            begin_pre(step)
                            project(bank, w_of[:, :, 2 * D:3 * D], xt[l], D).then_inc(pre_ready[l], 1)
                        elif name == "GATE":
                            begin_pre(step)
                            project(bank, wg0, xt[l], E).then_inc(pre_ready[l], 1)
                        elif name == "CT":
                            pe.wait_ge(top_done[l], it + 1)
                            begin_pre(step)
                            for t in range(NT):
                                last = pe.transpose(bank[0:E, t * P:(t + 1) * P], comb[l][:, t, :], ident[:, :])
                            last.then_inc(pre_ready[l], 1)
                        elif name == "MBIAS":
                            begin_pre(step)
                            for t in range(NT):
                                last = pe.matmul(bank[:, t * D:(t + 1) * D], combt[l][:, t * P:(t + 1) * P], bexp[:, :], start=True, stop=True)
                            last.then_inc(pre_ready[l], 1)
                        elif name == "EXPERT":
                            t, e = k
                            begin_pre(step)
                            for c in range(DC):
                                last = pe.matmul(bank[:, :], xt[l][:, c, t * P:(t + 1) * P],
                                                 wexp[:, c, e:e + 2, :].rearrange("p e n -> p (e n)"), start=c == 0, stop=c == DC - 1)
                            last.then_inc(pre_ready[l], 1)
                        elif name == "OTT":
                            pe.wait_ge(tr_read, it * N_TR + o_done(l, u))
                            begin_pre(step)
                            turn_tokens(bank, o[l]).then_inc(pre_ready[l], 1)
                        elif name == "PROJ":
                            begin_pre(step)
                            project(bank, wproj if u == 2 else wo, xt[l], D).then_inc(pre_ready[l], 1)
                        elif name == "S":
                            n = S_AT[step]
                            h, src = k
                            if h == 0 and src == 0:
                                pe.wait_ge(q_rows[l], (it * 4 + u + 1) * 16 * STACK_DMAS)
                                pe.wait_ge(k_rows[l], (it * 4 + u + 1) * 16 * STACK_DMAS)
                            pe.wait_ge(s_read, it * N_S + n + 1)
                            dst = s_ps[n % 2]
                            rows = BIAS if u == 0 else PRODUCTS
                            q = lambda t: qs[l][0:rows, h, t * P:(t + 1) * P]
                            if u == 2:
                                pe.matmul(dst[:, 0:T], q(src), kc[l][0:rows, h, :], start=True, stop=True)
                                last = pe.matmul(dst[:, T:2 * T], q(src), ks[l][0:rows, h, :], start=True, stop=True)
                            elif u == 3:
                                pe.matmul(dst[:, 0:P], q(0), ks[l][0:rows, h, 0:P], start=True, stop=False)
                                pe.matmul(dst[:, 0:P], ident_b[:, :], late_k[:, :], start=False, stop=True)
                                pe.matmul(dst[:, P:3 * P], q(1), ks[l][0:rows, h, :], start=True, stop=False)
                                last = pe.matmul(dst[:, 2 * P:3 * P], ident_b[:, :], late_k[:, :], start=False, stop=True)
                            else:
                                kst = kc[l] if u == 0 else ks[l]
                                for t in range(NT):
                                    last = pe.matmul(dst[:, t * T:(t + 1) * T], q(t), kst[0:rows, h, :], start=True, stop=True)
                            last.then_inc(s_ready, 1)
                        elif name == "MT":
                            pe.wait_ge(m_ready, it * N_M + M_AT[("M", l, u, k)] + 1)
                            pe.wait_ge(tr_read, it * N_TR + TR_AT[step] + 1)
                            for t in range(NT):
                                last = pe.transpose(tr_b[0:3 * HG, t * P:(t + 1) * P],
                                                    mp[l][k][:, t, :, :].rearrange("p a b -> p (a b)"), ident_b[:, :])
                            last.then_inc(tr_ready, 1)
                        elif name == "T":
                            n = T_AT[step]
                            h, src = k
                            if h % HG == 0 and src == 0:
                                pe.wait_ge(max_rows[l][h // HG], (it * 4 + u + 1) * 48)
                                if u == 2 and h == 0:
                                    pe.wait_ge(unbiased[l], it + 1)
                            pe.wait_ge(t_read, it * N_T + n + 1)
                            dst = t_ps[n % 2]
                            kst = kc[l] if u == 0 or (u == 2 and src == 0) else ks[l]
                            if u == 3:
                                pe.matmul(dst[:, 0:T], kst[0:ROWS, h, 0:P], qs[l][0:ROWS, h, :], start=True, stop=False)
                                pe.matmul(dst[:, 0:P], ident_b[:, :], late_q[:, :], start=False, stop=True)
                                pe.matmul(dst[:, T:T + P], kst[0:ROWS, h, P:T], qs[l][0:ROWS, h, P:T], start=True, stop=False)
                                last = pe.matmul(dst[:, T:T + P], ident_b[:, :], late_q[:, :], start=False, stop=True)
                            else:
                                for t in range(NT):
                                    last = pe.matmul(dst[:, t * T:(t + 1) * T], kst[0:ROWS, h, t * P:(t + 1) * P],
                                                     qs[l][0:ROWS, h, :], start=True, stop=True)
                            last.then_inc(t_ready, 1)
                        elif name == "PV":
                            v = PV_AT[step]
                            srcs = 2 if u == 2 else 1
                            slots = {(j, s): ("T", l, u, (k * QH + j, s)) for j in range(QH) for s in range(srcs)}
                            pe.wait_ge(t_read, it * N_T + max(T_AT[s] for s in slots.values()) + 3)
                            if k == 0:
                                if u in (0, 2):
                                    pe.wait_ge(vc_ready[l], it + 1)
                                if u:
                                    pe.wait_ge(pre_read[l], it * N_PRE + pre_done(("V", l, u, 0)))
                            pe.wait_ge(pv_read, it * N_PV + v + 1)
                            for s in range(srcs):
                                val = vc[l] if u == 0 or (u == 2 and s == 0) else va[l]
                                for t in range(NT):
                                    q0 = P if u == 3 and t == 1 else 0
                                    for j in range(QH):
                                        e = ex[l][:, EX_AT[slots[(j, s)]] % EXPS, t * T:t * T + T - q0]
                                        last = pe.matmul(pv_ps[j * VW:(j + 1) * VW, q0:T], val[:, t, k * QH + j, :], e,
                                                         start=s == 0 and t == 0, stop=s == srcs - 1 and t == NT - 1,
                                                         tile_position=(0, j * VW))
                            last.then_inc(pv_ready, 1)
                        elif name == "OT":
                            v = PV_AT[("PV", l, u, k)]
                            pe.wait_ge(pv_read, it * N_PV + v + 2)
                            pe.wait_ge(tr_read, it * N_TR + TR_AT[step] + 1)
                            for t in range(NT):
                                last = pe.transpose(tr_ps[:, t * P:(t + 1) * P], ot[v % 2][:, t * P:(t + 1) * P], ident[:, :])
                            last.then_inc(tr_ready, 1)

                stages(HEAD, -1)
                with pe.Fori(0, TURNS) as turn:
                    stages(STEPS, turn)

            @block.scalar
            def _(act):
                def stages(steps, turn):
                    def produced(step):
                        act.wait_ge(pre_ready[step[1]], it * N_PRE + PRE_AT[step] + 1)

                    for step in steps:
                        it = turn_of(step, turn)
                        name, l, u, k = step
                        bank = pre_ps[l]
                        flat = lambda z: z[:, :, :].rearrange("p a b -> p (a b)")
                        if name in ("XT", "KT", "OTT"):
                            produced(step)
                            dst = ak[l] if name == "KT" else aq[l] if u == 0 else xt[l]
                            by = SCALE if name == "XT" and u == 0 else 1.0
                            last = act.activation(flat(dst), bank[:, :], ACT.Copy, scale=by)
                            if u == 0:
                                part = pk[l][:, :, 2, :] if name == "KT" else pq[l][:, :, 0, :]
                                last = act.activation(part, bank[:, :].rearrange("p (c t) -> p c t", c=DC), ACT.Copy, scale=by)
                            last.then_inc(pre_read[l], 1)
                        elif name in ("Q", "K"):
                            produced(step)
                            dst, part = (aq[l], pq[l][:, :, 0, :]) if name == "Q" else (ak[l], pk[l][:, :, 2, :])
                            by = SCALE if name == "Q" else 1.0
                            for z in (dst, part):
                                if u == 1:
                                    for c in range(DC):
                                        col = c if name == "Q" else DC + c
                                        last = act.activation(z[:, c, :], bank[:, c * T:(c + 1) * T], ACT.Identity,
                                                              bias=bqk[:, col:col + 1], scale=by)
                                else:
                                    last = act.activation(z[:, :, :], bank[:, :].rearrange("p (c t) -> p c t", c=DC), ACT.Copy, scale=by)
                            last.then_inc(pre_read[l], 1)
                        elif name == "V" and u > 1:
                            produced(step)
                            act.activation(va[l][:, :, :, 0:HD], bank[:, :].rearrange("p (t h d) -> p t h d", t=NT, h=H),
                                           ACT.Copy).then_inc(pre_read[l], 1)
                        elif name == "CT":
                            produced(step)
                            act.activation(combt[l][:, :], bank[0:E, 0:T], ACT.Copy).then_inc(pre_read[l], 1)
                        elif name == "GEXP":
                            act.wait_ge(lg_ready[l], it + 1)
                            act.activation(flat(pr[l]), flat(lg[l]), ACT.Exp).then_inc(lg_exp[l], 1)
                        elif name == "MT":
                            act.wait_ge(tr_ready, it * N_TR + TR_AT[step] + 1)
                            act.activation(mt[l][k][:, :], tr_b[0:3 * HG, 0:T], ACT.Copy).then_inc(tr_read, 1)
                        elif name == "T":
                            n = T_AT[step]
                            act.wait_ge(t_ready, it * N_T + n + 1)
                            w = 3 * P if u == 3 else 2 * T
                            act.activation(ex[l][:, EX_AT[step] % EXPS, 0:w], t_ps[n % 2][:, 0:w], ACT.Exp).then_inc(t_read, 1)
                        elif name == "PV":
                            v = PV_AT[step]
                            act.wait_ge(pv_ready, it * N_PV + v + 1)
                            act.activation(ot[v % 2][:, :], pv_ps[:, 0:T], ACT.Copy).then_inc(pv_read, 1)

                stages(HEAD, -1)
                with act.Fori(0, TURNS) as turn:
                    stages(STEPS, turn)

            @block.gpsimd
            def _(pool):
                def stages(steps, turn):
                    s = Steps(pool, pool_done, max(turn, 0) if isinstance(turn, int) else turn, POOL_STEPS, pool_passed, 1 if steps is HEAD else 1 + POOL_HEAD)
                    for step in steps:
                        it = turn_of(step, turn)
                        name, l, u, k = step
                        if name == "LOAD":
                            pool.wait_ge(x_loaded[l], it * 80 + 80)
                            s.wait_alone()
                            s.done(pool.tensor_copy(vc[l][:, :, :, 0:HD], ctx[l][:, :, D:2 * D].rearrange("p t (h d) -> p t h d", h=H)))
                            s.wait()
                            pool.sem_inc(vc_ready[l], 1)
                        elif name == "KSPLIT":
                            s.wait()
                            pool.wait_ge(pre_read[l], it * N_PRE + pre_done(("KT" if u == 0 else "K", l, u, 0)))
                            s.done(pool.tensor_tensor(ak[l][:, :, :], ak[l][:, :, :], pk[l][:, :, 2, :], ALU.subtract))
                            s.wait_alone()
                            s.done(pool.tensor_copy(pk[l][:, :, 1, :], ak[l][:, :, :]))
                            s.wait()
                            s.done(pool.tensor_tensor(pk[l][:, :, 0, :], ak[l][:, :, :], pk[l][:, :, 1, :], ALU.subtract))
                            s.wait()
                            pool.sem_inc(k_split[l], 1)
                        elif name == "UNBIAS":
                            pool.wait_ge(tr_read, it * N_TR + o_done(l, 0))
                            s.wait_alone()
                            s.done(pool.memset(kc[l][PRODUCTS:BIAS, :, :], 0.0))
                            s.wait()
                            pool.sem_inc(unbiased[l], 1)
                    assert s.n == (POOL_HEAD if steps is HEAD else POOL_STEPS), s.n

                stages(HEAD, -1)
                with pool.Fori(0, TURNS) as turn:
                    stages(STEPS, turn)

            @block.vector
            def _(dve):
                def stages(steps, turn):
                    s = Steps(dve, dve_step, max(turn, 0) if isinstance(turn, int) else turn, DVE_STEPS, dve_passed, 0 if steps is HEAD else DVE_HEAD)
                    flat = lambda z: z[:, :, :].rearrange("p a b -> p (a b)")
                    wide = lambda z: z[:, :].unsqueeze(2).broadcast_to([P, NT, E])

                    def produced(step):
                        dve.wait_ge(pre_ready[step[1]], it * N_PRE + PRE_AT[step] + 1)

                    for step in steps:
                        it = turn_of(step, turn)
                        name, l, u, k = step
                        bank = pre_ps[l]
                        if name == "LN" and k == 0:
                            if u == 0:
                                dve.wait_ge(x_loaded[l], it * 80 + 80)
                            else:
                                if u < 3:
                                    dve.wait_ge(tr_read, it * N_TR + o_done(l, u - 1))
                                if u == 2:
                                    s.wait()
                                    s.done(dve.tensor_tensor(flat(o[l]), flat(o[l]), flat(moe[l]), ALU.add))
                                    s.wait()
                                if u < 3:
                                    gate = (0, 2)[u - 1]
                                    s.done(dve.scalar_tensor_tensor(out=flat(xs[l]), in0=flat(o[l]), scalar=tanh_g[:, gate:gate + 1],
                                                                    in1=flat(xs[l]), op0=ALU.mult, op1=ALU.add))
                                s.wait()
                            for t in range(NT):
                                s.done(dve.bn_stats(stats[l][:, t, :], xs[l][:, t, :]))
                            s.wait_alone()
                            for t in range(NT):
                                s.done(dve.bn_aggr(mv[l][:, t, :], stats[l][:, t, :]))
                        elif name == "LN":
                            s.wait()
                            if k == 1:
                                root_guess(dve, s, mv[l][:, :, 1], rstd[l][:, :], root_v[l][:, :])
                            elif k < SUBSTEPS["LN"] - 1:
                                root_step(dve, s, rstd[l][:, :], root_v[l][:, :], root_w[l][:, :])
                            else:
                                for t in range(NT):
                                    last = dve.tensor_scalar(xn[l][:, t, :], xs[l][:, t, :], mv[l][:, t, 0:1], rstd[l][:, t:t + 1],
                                                             ALU.subtract, ALU.mult)
                                    if t < NT - 1:
                                        s.done(last)
                                last.then_inc(xn_ready[l], 1)
                        elif name == "QSPLIT":
                            dve.wait_ge(pre_read[l], it * N_PRE + pre_done(("XT" if u == 0 else "Q", l, u, 0)))
                            s.done(dve.tensor_tensor(aq[l][:, :, :], aq[l][:, :, :], pq[l][:, :, 0, :], ALU.subtract))
                            s.wait()
                            s.done(dve.tensor_copy(pq[l][:, :, 1, :], aq[l][:, :, :]))
                            s.wait()
                            dve.tensor_tensor(pq[l][:, :, 2, :], aq[l][:, :, :], pq[l][:, :, 1, :], ALU.subtract).then_inc(q_split[l], 1)
                        elif name == "V" and u == 1:
                            produced(step)
                            dve.tensor_tensor(va[l][:, :, :, 0:HD], bank[:, :].rearrange("p (t h d) -> p t h d", t=NT, h=H),
                                              bv[:, :].rearrange("p (h d) -> p h d", h=H).unsqueeze(1).broadcast_to([P, NT, H, HD]),
                                              ALU.add).then_inc(pre_read[l], 1)
                        elif name == "S":
                            n = S_AT[step]
                            h, src = k
                            dve.wait_ge(s_ready, it * N_S + n + 1)
                            dst, w = (mx3[l][:, h, :], 3 * P) if u == 3 else (mx[l][:, h, src:src + 1], 2 * T) if u == 2 else (mx[l][:, h, :], 2 * T)
                            parts = dst.shape[-1]
                            dve.tensor_reduce(dst, s_ps[n % 2][:, 0:w].rearrange("p (a b) -> p a b", a=parts), AX.X, ALU.max).then_inc(s_read, 1)
                        elif name == "M":
                            srcs = 2 if u == 2 else 1
                            hs = slice(k * HG, (k + 1) * HG)
                            dve.wait_ge(s_read, it * N_S + S_AT[("S", l, u, (k * HG + HG - 1, srcs - 1))] + 3)
                            if u == 3:
                                s.done(dve.tensor_copy(mx[l][:, hs, 0], mx3[l][:, hs, 0]))
                                s.done(dve.tensor_tensor(mx[l][:, hs, 1], mx3[l][:, hs, 1], mx3[l][:, hs, 2], ALU.max))
                                s.wait()
                            m = mx[l][:, hs, :].rearrange("p h t -> p t h")
                            part = [mp[l][k][:, :, j, :] for j in range(3)]
                            s.done(dve.tensor_scalar(part[0], m, -1.0, None, ALU.mult))
                            s.wait()
                            s.done(dve.scalar_tensor_tensor(out=mr[:, :, :], in0=m, scalar=-1.0, in1=part[0], op0=ALU.mult, op1=ALU.subtract))
                            s.wait()
                            s.done(dve.tensor_copy(part[1], mr[:, :, :]))
                            s.wait()
                            dve.tensor_tensor(part[2], mr[:, :, :], part[1], ALU.subtract).then_inc(m_ready, 1)
                        elif name == "OT":
                            dve.wait_ge(tr_ready, it * N_TR + TR_AT[step] + 1)
                            heads = tr_ps[:, 0:T].rearrange("p (t j w) -> p t j w", t=NT, j=QH)
                            s.done(dve.reciprocal(rden[:, :, :], heads[:, :, :, HD]))
                            s.wait()
                            dve.tensor_tensor(o[l][:, :, k * QH * HD:(k + 1) * QH * HD].rearrange("p t (j d) -> p t j d", j=QH), heads[:, :, :, 0:HD],
                                              rden[:, :, :].unsqueeze(3).broadcast_to([P, NT, QH, HD]), ALU.mult).then_inc(tr_read, 1)
                        elif name == "GATE":
                            produced(step)
                            logits = bank[:, 0:NT * E].rearrange("p (t e) -> p t e", t=NT)
                            last = dve.tensor_tensor(lg[l][:, :, :], logits, bg0[:, :].unsqueeze(1).broadcast_to([P, NT, E]), ALU.add)
                            last.then_inc(pre_read[l], 1)
                            dve.wait_ge(pre_read[l], it * N_PRE + pre_done(step))
                            s.done(dve.tensor_reduce(t1[0][l][:, :], lg[l][:, :, :], AX.X, ALU.max))
                            s.wait()
                            dve.tensor_tensor(lg[l][:, :, :], lg[l][:, :, :], wide(t1[0][l]), ALU.subtract).then_inc(lg_ready[l], 1)
                        elif name == "TOP":
                            j, part = divmod(k - 1, 2)
                            hot = t8[1 + j % 2][l]
                            if k == 0:
                                dve.wait_ge(lg_exp[l], it + 1)
                                s.done(dve.tensor_reduce(t1[0][l][:, :], pr[l][:, :, :], AX.X, ALU.add))
                                s.wait()
                                s.done(dve.reciprocal(t1[1][l][:, :], t1[0][l][:, :]))
                                s.wait()
                                s.done(dve.tensor_tensor(pr[l][:, :, :], pr[l][:, :, :], wide(t1[1][l]), ALU.mult))
                            elif k < 5 and part == 0:
                                left = pr[l] if j == 0 else t8[0][l]
                                s.wait()
                                s.done(dve.tensor_reduce(t1[j][l][:, :], left[:, :, :], AX.X, ALU.max))
                                s.wait()
                                s.done(dve.tensor_tensor(hot[:, :, :], left[:, :, :], wide(t1[j][l]), ALU.is_equal))
                                s.wait()
                                s.done(dve.tensor_tensor(hot[:, :, :], hot[:, :, :], first[:, :, :], ALU.mult))
                            elif k < 5:
                                s.wait()
                                s.done(dve.tensor_reduce(t1[2][l][:, :], hot[:, :, :], AX.X, ALU.max))
                                s.wait()
                                s.done(dve.tensor_tensor(hot[:, :, :], hot[:, :, :], wide(t1[2][l]), ALU.is_equal))
                                if j == 0:
                                    s.wait()
                                    s.done(dve.scalar_tensor_tensor(out=flat(t8[0][l]), in0=flat(hot), scalar=-2.0, in1=flat(pr[l]),
                                                                    op0=ALU.mult, op1=ALU.add))
                            else:
                                s.wait()
                                s.done(dve.tensor_tensor(flat(t8[0][l]), flat(t8[1][l]), flat(t8[2][l]), ALU.add))
                                s.wait()
                                dve.tensor_tensor(comb[l][:, :, :], pr[l][:, :, :], t8[0][l][:, :, :], ALU.mult).then_inc(top_done[l], 1)
                        elif name == "MBIAS":
                            produced(step)
                            dve.tensor_copy(flat(moe[l]), bank[:, :]).then_inc(pre_read[l], 1)
                        elif name == "EXPERT":
                            t, e = k
                            produced(step)
                            if e == 0:
                                dve.wait_ge(pre_read[l], it * N_PRE + pre_done(("MBIAS", l, u, 0)))
                                dve.wait_ge(top_done[l], it + 1)
                            for j in range(2):
                                s.wait()
                                last = dve.scalar_tensor_tensor(out=moe[l][:, t, :], in0=bank[:, j * D:(j + 1) * D], scalar=comb[l][:, t, e + j:e + j + 1],
                                                                in1=moe[l][:, t, :], op0=ALU.mult, op1=ALU.add)
                                if j == 0:
                                    s.done(last)
                            last.then_inc(pre_read[l], 1)
                            dve.wait_ge(pre_read[l], it * N_PRE + pre_done(step))
                        elif name == "PROJ":
                            produced(step)
                            if u == 2:
                                dve.scalar_tensor_tensor(out=flat(xs[l]), in0=bank[:, :], scalar=tanh_g[:, 1:2], in1=flat(xs[l]),
                                                         op0=ALU.mult, op1=ALU.add).then_inc(pre_read[l], 1)
                                dve.wait_ge(pre_read[l], it * N_PRE + pre_done(step))
                                s.done(dve.tensor_tensor(xs[l][:, :, :], xs[l][:, :, :], bproj[:, :].unsqueeze(1).broadcast_to([P, NT, D]), ALU.add))
                            else:
                                dve.tensor_tensor(flat(o[l]), bank[:, :], flat(xn[l]), ALU.add).then_inc(pre_read[l], 1)
                    assert s.n == (DVE_HEAD if steps is HEAD else DVE_STEPS), s.n

                stages(HEAD, -1)
                with dve.Fori(0, TURNS) as turn:
                    stages(STEPS, turn)


def expert_phase(nc, a):
    keep, weights = ExitStack(), ExitStack()
    e = dict(a)
    with keep:
        e["share_of"] = keep.enter_context(nc.sbuf_tensor("share_of", [P, TILES, TOPK], F32))
        with weights:
            sb = lambda name, shape, dt=F32: weights.enter_context(nc.sbuf_tensor(name, shape, dt))
            e["wup"], e["wdn"] = sb("wup", [P, DC, E, F]), sb("wdn", [P, E, FC, D])
            e["bup"], e["bdn"] = sb("bup", [P, E, F]), sb("bdn", [P, E, D])
            e["expert_of"] = sb("expert_of", [P, COLS], I32)
            e["row_of"] = sb("row_of", [P, COLS], I32)
            e["dest_of"] = sb("dest_of", [P, COLS], U32)
            e["w_loaded"] = weights.enter_context(nc.semaphore("ew_loaded"))
            route(nc, e)
            run_experts(nc, e)
        combine(nc, e)


def pair(d, first):
    return d[bass.ds(first, 2)].rearrange("b p t n -> p b (t n)")


def flat_pair(z):
    return z[:, :, :].rearrange("p (b t) n -> p b (t n)", b=2)


def wait_alone(eng, sem, value, passed):
    eng.wait_ge(sem, value)
    eng.sem_inc(passed, 1)


def route(nc, a):
    own = ExitStack()
    with own:
        sb = lambda name, shape, dt=F32: own.enter_context(nc.sbuf_tensor(name, shape, dt))
        sem = lambda name: own.enter_context(nc.semaphore(name))
        ps = lambda name, w=512: own.enter_context(nc.psum_tensor(name, [P, w], F32))
        two, ring = range(2), range(RING)
        ident, share_of, expert_of, row_of, dest_of = a["ident"], a["share_of"], a["expert_of"], a["row_of"], a["dest_of"]
        g1 = sb("r_g1", [P, D]); b1 = sb("r_b1", [P, D]); wg1 = sb("r_wg1", [P, DC, E])
        hb = [sb(f"r_h{q}", [P, QT, D]) for q in ring]; ht = [sb(f"r_ht{q}", [P, DC, QT * P]) for q in two]
        stats = sb("r_stats", [P, QT, 6]); mv = sb("r_mv", [P, QT, 2])
        rstd = [sb(f"r_rstd{q}", [P, QT]) for q in ring]; shift = [sb(f"r_shift{q}", [P, QT]) for q in ring]
        root_v = sb("r_root_v", [P, QT]); root_w = sb("r_root_w", [P, QT])
        pr = sb("r_pr", [P, TILES, E])
        z8 = [sb(f"r_z8_{k}", [P, TILES, E]) for k in range(5)]
        z1 = [sb(f"r_z1_{k}", [P, TILES]) for k in range(4)]
        ones = sb("r_ones", [P, P]); before = sb("r_before", [P, P])
        first = sb("r_first", [P, E]); tile_i = sb("r_tile_i", [P, COLS], I32); tile_f = sb("r_tile_f", [P, COLS])
        past = hb[2][:, :, :].rearrange("p t n -> p (t n)")[:, 0:COLS * E].rearrange("p (c e) -> p c e", e=E); ended = sb("r_ended", [P, COLS])
        n8 = [sb(f"r_n8_{k}", [P, E]) for k in range(4)]; n8i = sb("r_n8i", [P, E], I32)
        lane_i = sb("r_lane_i", [P, P], I32); lane_f = sb("r_lane_f", [P, P])
        name_i = sb("r_name_i", [P, TILES], I32); name = [sb(f"r_name{j}", [P, TILES]) for j in range(TOPK)]
        slot_i = sb("r_slot_i", [P, TILES], I32); tile_at = sb("r_tile_at", [P, TILES]); row_at = sb("r_row_at", [P, TILES])
        CHUNK = DC * QT
        PARTS = TILES // CHUNK
        row_hot = [ht[k][:, :, :].rearrange("p c (t n) -> p (c t) n", n=P) for k in two]; tile_hot = [hb[k][:, :, :].rearrange("p t n -> p (t n)")[:, 0:CHUNK * COLS].rearrange("p (t c) -> p t c", c=COLS) for k in two]
        named = sb("r_named", [P, COLS]); dest = sb("r_dest", [P, COLS]); row_i = sb("r_row_i", [P, COLS], I32)
        t_ps = [ps(f"r_t_ps{q}", 2 * 512) for q in two]; g_ps = [ps(f"r_g_ps{q}") for q in two]
        rank_ps, count_ps = ps("r_rank_ps"), ps("r_count_ps")
        name_ps = g_ps[0]
        small, consts, step, passed, first_ready = sem("r_small"), sem("r_consts"), sem("r_step"), sem("r_passed"), sem("r_first_ready")
        loaded, moments, normed, h_ready, h_stored = ([sem(f"r_{n}{q}") for q in ring] for n in ("loaded", "moments", "normed", "h_ready", "h_stored"))
        turned, ht_copied, g_ready, g_read = ([sem(f"r_{n}{q}") for q in two] for n in ("turned", "ht_copied", "g_ready", "g_read"))
        hot_ready, ranked, slots_hot, slots_named, lg_ready, lg_exp, sp_passed = (
            sem(f"r_{n}") for n in ("hot_ready", "ranked", "slots_hot", "slots_named", "lg_ready", "lg_exp", "sp_passed"))

        with nc.Block() as block:
            @block.sync
            def _(sp):
                sp.dma_start(g1[:, :], a["ln1_g"].partition_broadcast(P)).then_inc(small, 16)
                sp.dma_start(b1[:, :], a["ln1_b"].partition_broadcast(P)).then_inc(small, 16)
                sp.dma_start(wg1[:, :, :], a["w1_gate"].rearrange("(c p) n -> p c n", p=P)).then_inc(small, 16)
                for q in ring:
                    sp.sem_inc(h_stored[q], 16)
                for q in two:
                    sp.sem_inc(turned[q], 2)
                    sp.sem_inc(ht_copied[q], 1)
                    sp.sem_inc(g_read[q], 1)

            @block.gpsimd
            def _(pool):
                pool.memset(ones[:, :], 1.0).then_inc(consts, 1)
                pool.memset(before[:, :], 1.0).then_inc(consts, 1)
                pool.iota(tile_i[:, :], pattern=[[1, COLS]], base=0, channel_multiplier=0).then_inc(consts, 1)
                pool.iota(lane_i[:, :], pattern=[[1, P]], base=0, channel_multiplier=0).then_inc(consts, 1)
                pool.iota(name_i[:, :].rearrange("p (b t) -> p b t", b=B), pattern=[[P * NT * TOPK, B], [TOPK, NT]], base=1,
                          channel_multiplier=NT * TOPK).then_inc(consts, 1)
                pool.wait_ge(consts, 5)
                pool.affine_select(out=before[:, :], in_=before[:, :], compare_op=ALU.is_ge, fill=0.0, base=-1,
                                   pattern=[[1, P]], channel_multiplier=-1).then_inc(consts, 1)

            @block.vector
            def _(dve):
                for k in range(E):
                    last = dve.memset(first[:, k:k + 1], float(E - k))
                last.then_inc(first_ready, 1)
                dve.wait_ge(first_ready, 1)
                dve.wait_ge(small, 48)
                dve.wait_ge(consts, 6)

        with nc.Block() as block:
            @block.scalar
            def _(act):
                with act.Fori(0, PAIRS // RING) as it:
                    def copy_turned(q, x):
                        act.wait_ge(turned[q % 2], it * (RING // 2) + q // 2 + 3)
                        for c in range(DC):
                            last = act.activation(ht[q % 2][:, c, :], t_ps[q % 2][:, c * 512:(c + 1) * 512], ACT.Copy)
                        last.then_inc(ht_copied[q % 2], 1)
                        for c in range(DC):
                            act.dma_start(a["wup"][:, c, bass.ds(x, 1), :], a["w_up"][bass.ds(x, 1), c * P:(c + 1) * P, :].rearrange("o p n -> p o n")).then_inc(a["w_loaded"], 16)
                        act.dma_start(a["wdn"][:, bass.ds(x, 1), :, :].rearrange("p o f n -> p (o f) n"),
                                      a["w_down"][bass.ds(x, 1)].rearrange("o (f p) n -> p (o f) n", p=P)).then_inc(a["w_loaded"], 16)

                    expert = [act.snap(it * RING + q) for q in ring]
                    for q in ring:
                        act.wait_ge(moments[q], it + 1)
                        for t in range(QT):
                            last = act.activation(hb[q][:, t, :], hb[q][:, t, :], ACT.Identity, bias=shift[q][:, t:t + 1], scale=rstd[q][:, t:t + 1])
                        last.then_inc(normed[q], 1)
                        if q:
                            copy_turned(q - 1, expert[q - 1])
                    copy_turned(RING - 1, expert[RING - 1])
                act.dma_start(a["bup"][:, :, :].rearrange("p e f -> p (e f)"), a["b_up"].rearrange("e f -> (e f)").partition_broadcast(P)).then_inc(a["w_loaded"], 16)
                act.dma_start(a["bdn"][:, :, :].rearrange("p e f -> p (e f)"), a["b_down"].rearrange("e f -> (e f)").partition_broadcast(P)).then_inc(a["w_loaded"], 16)
                act.wait_ge(lg_ready, 1)
                act.activation(pr[:, :, :].rearrange("p a b -> p (a b)"), z8[0][:, :, :].rearrange("p a b -> p (a b)"), ACT.Exp).then_inc(lg_exp, 1)

            @block.sync
            def _(sp):
                with sp.Fori(0, PAIRS // RING) as it:
                    for q in ring:
                        free, gone, first = sp.snap(it * 16 + 16), sp.snap(it * (RING // 2) + q // 2 + 1), sp.snap(it * 2 * RING + q * 2)
                        wait_alone(sp, h_stored[q], free, sp_passed)
                        wait_alone(sp, turned[q % 2], gone, sp_passed)
                        sp.dma_start(flat_pair(hb[q]), pair(a["h_d"], first)).then_inc(loaded[q], 16)
                    for q in ring:
                        normed_rows, first = sp.snap(it + 1), sp.snap(it * 2 * RING + q * 2)
                        wait_alone(sp, h_ready[q], normed_rows, sp_passed)
                        sp.dma_start(pair(a["hn_d"], first), flat_pair(hb[q])).then_inc(h_stored[q], 16)
                for q in ring:
                    sp.wait_ge(h_stored[q], 16 * (PAIRS // RING + 1))

            @block.tensor
            def _(pe):
                with pe.Fori(0, PAIRS // RING) as it:
                    def logits(q):
                        r, use = q % 2, it * (RING // 2) + q // 2
                        pe.wait_ge(ht_copied[r], use + 2)
                        pe.wait_ge(g_read[r], use + 1)
                        for t in range(QT):
                            for c in range(DC):
                                last = pe.matmul(g_ps[r][:, t * E:(t + 1) * E], ht[r][:, c, t * P:(t + 1) * P], wg1[:, c, :], start=c == 0, stop=c == DC - 1)
                        last.then_inc(g_ready[r], 1)

                    for q in ring:
                        r, use = q % 2, it * (RING // 2) + q // 2
                        pe.wait_ge(h_ready[q], it + 1)
                        pe.wait_ge(ht_copied[r], use + 1)
                        for c in range(DC):
                            for t in range(QT):
                                last = pe.transpose(t_ps[r][:, c * 512 + t * P:c * 512 + (t + 1) * P], hb[q][:, t, c * P:(c + 1) * P], ident[:, :])
                        last.then_inc(turned[r], 1)
                        if q:
                            logits(q - 1)
                    logits(RING - 1)
                pe.wait_ge(hot_ready, 1)
                hot = z8[3][:, :, :].rearrange("p a b -> p (a b)")
                pe.matmul(rank_ps[:, 0:TILES * E], before[:, :], hot, start=True, stop=True)
                pe.matmul(count_ps[:, 0:TILES * E], ones[:, :], hot, start=True, stop=True).then_inc(ranked, 1)
                for k in range(TOPK * PARTS):
                    pe.wait_ge(slots_hot, k + 1)
                    for t in range(CHUNK):
                        last = pe.matmul(name_ps[:, 0:COLS], row_hot[k % 2][:, t, :], tile_hot[k % 2][:, t, :],
                                         start=k == 0 and t == 0, stop=k == TOPK * PARTS - 1 and t == CHUNK - 1)
                    last.then_inc(slots_named, 1)

            @block.vector
            def _(dve):
                with dve.Fori(0, PAIRS // RING) as it:
                    s = Steps(dve, step, it, ROUTE_STEPS, passed)
                    row = lambda z: z[:, :].unsqueeze(1).broadcast_to([P, QT, D])

                    def scale_rows(q):
                        dve.wait_ge(normed[q], it + 1)
                        s.done(dve.tensor_tensor(hb[q][:, :, :], hb[q][:, :, :], row(g1), ALU.mult))
                        s.wait()
                        dve.tensor_tensor(hb[q][:, :, :], hb[q][:, :, :], row(b1), ALU.add).then_inc(h_ready[q], 1)

                    def keep_logits(q):
                        dve.wait_ge(g_ready[q % 2], it * (RING // 2) + q // 2 + 1)
                        s.stand()
                        dve.tensor_copy(pr[:, bass.ds(it * RING * QT + q * QT, QT), :],
                                        g_ps[q % 2][:, 0:QT * E].rearrange("p (t e) -> p t e", e=E)).then_inc(g_read[q % 2], 1)

                    for q in ring:
                        dve.wait_ge(loaded[q], it * 16 + 16)
                        norm_moments(dve, s, hb[q], stats, mv, rstd[q], root_v, root_w, QT)
                        dve.scalar_tensor_tensor(out=shift[q][:, :], in0=mv[:, :, 0], scalar=-1.0, in1=rstd[q][:, :],
                                                 op0=ALU.mult, op1=ALU.mult).then_inc(moments[q], 1)
                        if q:
                            scale_rows(q - 1)
                        if q > 1:
                            keep_logits(q - 2)
                    scale_rows(RING - 1)
                    keep_logits(RING - 2)
                    keep_logits(RING - 1)
                    assert s.n == ROUTE_STEPS, s.n
                for q in two:
                    dve.wait_ge(g_read[q], PAIRS // 2 + 1)
                for q in ring:
                    dve.wait_ge(h_stored[q], 16 * (PAIRS // RING + 1))
                s = Steps(dve, step, 1, ROUTE_STEPS * (PAIRS // RING), passed)
                wide = lambda z: z[:, :].unsqueeze(2).broadcast_to([P, TILES, E])
                tall = lambda z: z[:, :].unsqueeze(1).broadcast_to([P, TILES, E])
                full = lambda z: z[:, :, :]

                def then(ins):
                    s.done(ins)
                    s.wait()

                then(dve.tensor_reduce(z1[0][:, :], full(pr), AX.X, ALU.max))
                dve.tensor_tensor(full(z8[0]), full(pr), wide(z1[0]), ALU.subtract).then_inc(lg_ready, 1)
                dve.wait_ge(lg_exp, 1)
                then(dve.tensor_reduce(z1[0][:, :], full(pr), AX.X, ALU.add))
                then(dve.reciprocal(z1[1][:, :], z1[0][:, :]))
                then(dve.tensor_tensor(full(pr), full(pr), wide(z1[1]), ALU.mult))
                for j in range(TOPK):
                    left, hot = pr if j == 0 else z8[0], z8[1 + j]
                    then(dve.tensor_reduce(z1[j][:, :], full(left), AX.X, ALU.max))
                    then(dve.tensor_tensor(full(hot), full(left), wide(z1[j]), ALU.is_equal))
                    then(dve.tensor_tensor(full(hot), full(hot), tall(first), ALU.mult))
                    then(dve.tensor_reduce(z1[2][:, :], full(hot), AX.X, ALU.max))
                    then(dve.tensor_tensor(full(hot), full(hot), wide(z1[2]), ALU.is_equal))
                    if j == 0:
                        then(dve.scalar_tensor_tensor(out=full(z8[0]), in0=full(hot), scalar=-2.0, in1=full(pr), op0=ALU.mult, op1=ALU.add))
                dve.tensor_tensor(full(z8[3]), full(z8[1]), full(z8[2]), ALU.add).then_inc(hot_ready, 1)
                then(dve.tensor_tensor(z1[2][:, :], z1[0][:, :], z1[1][:, :], ALU.add))
                then(dve.reciprocal(z1[3][:, :], z1[2][:, :]))
                for j in range(TOPK):
                    then(dve.tensor_tensor(share_of[:, :, j], z1[j][:, :], z1[3][:, :], ALU.mult))
                dve.wait_ge(ranked, 1)
                counts = count_ps[:, 0:TILES * E].rearrange("p (t e) -> p t e", e=E)
                then(dve.tensor_copy(full(z8[0]), counts))
                src, dst = z8[0], z8[4]
                far = 1
                while far < TILES:
                    then(dve.tensor_copy(dst[:, 0:far, :], src[:, 0:far, :]))
                    then(dve.tensor_tensor(dst[:, far:TILES, :], src[:, far:TILES, :], src[:, 0:TILES - far, :], ALU.add))
                    src, dst, far = dst, src, far * 2
                then(dve.tensor_scalar(n8[0][:, :], src[:, TILES - 1, :], float(P - 1), None, ALU.add))
                then(dve.tensor_copy(n8i[:, :], n8[0][:, :]))
                then(dve.tensor_scalar(n8i[:, :], n8i[:, :], P.bit_length() - 1, None, ALU.logical_shift_right))
                then(dve.tensor_copy(n8[0][:, :], n8i[:, :]))
                up_to, spare = n8[1], n8[2]
                then(dve.tensor_copy(up_to[:, :], n8[0][:, :]))
                far = 1
                while far < E:
                    then(dve.tensor_copy(spare[:, 0:far], up_to[:, 0:far]))
                    then(dve.tensor_tensor(spare[:, far:E], up_to[:, far:E], up_to[:, 0:E - far], ALU.add))
                    up_to, spare, far = spare, up_to, far * 2
                then(dve.tensor_copy(tile_f[:, :], tile_i[:, :]))
                many = [P, COLS, E]
                then(dve.tensor_tensor(full(past), up_to[:, :].unsqueeze(1).broadcast_to(many), tile_f[:, :].unsqueeze(2).broadcast_to(many), ALU.is_le))
                then(dve.tensor_reduce(ended[:, :], full(past), AX.X, ALU.add))
                then(dve.tensor_scalar(expert_of[:, :], ended[:, :], float(E - 1), None, ALU.min))
                then(dve.tensor_tensor(n8[3][:, :], up_to[:, :], n8[0][:, :], ALU.subtract))
                then(dve.tensor_scalar(n8[3][:, :], n8[3][:, :], float(P), 1.0, ALU.mult, ALU.add))
                then(dve.tensor_tensor(full(dst), full(src), counts, ALU.subtract))
                then(dve.tensor_tensor(full(dst), rank_ps[:, 0:TILES * E].rearrange("p (t e) -> p t e", e=E), full(dst), ALU.add))
                then(dve.tensor_tensor(full(dst), full(dst), tall(n8[3]), ALU.add))
                then(dve.tensor_copy(lane_f[:, :], lane_i[:, :]))
                then(dve.tensor_copy(name[0][:, :], name_i[:, :]))
                then(dve.tensor_scalar(name[1][:, :], name[0][:, :], 1.0, None, ALU.add))
                for j in range(TOPK):
                    then(dve.tensor_tensor(full(src), full(dst), full(z8[1 + j]), ALU.mult))
                    then(dve.tensor_reduce(z1[j][:, :], full(src), AX.X, ALU.add))
                    then(dve.tensor_scalar(z1[j][:, :], z1[j][:, :], -1.0, None, ALU.add))
                    then(dve.tensor_copy(slot_i[:, :], z1[j][:, :]))
                    then(dve.tensor_scalar(slot_i[:, :], slot_i[:, :], P.bit_length() - 1, None, ALU.logical_shift_right))
                    then(dve.tensor_copy(tile_at[:, :], slot_i[:, :]))
                    then(dve.scalar_tensor_tensor(out=row_at[:, :], in0=tile_at[:, :], scalar=-float(P), in1=z1[j][:, :], op0=ALU.mult, op1=ALU.add))
                    for part in range(PARTS):
                        k = j * PARTS + part
                        ts = slice(part * CHUNK, (part + 1) * CHUNK)
                        if k >= 2:
                            dve.wait_ge(slots_named, k - 1)
                        over = lambda z, n: z[:, ts].unsqueeze(2).broadcast_to([P, CHUNK, n])
                        each = lambda z, n: z[:, :].unsqueeze(1).broadcast_to([P, CHUNK, n])
                        s.done(dve.tensor_tensor(full(row_hot[k % 2]), over(row_at, P), each(lane_f, P), ALU.is_equal))
                        then(dve.tensor_tensor(full(tile_hot[k % 2]), over(tile_at, COLS), each(tile_f, COLS), ALU.is_equal))
                        dve.tensor_tensor(full(tile_hot[k % 2]), full(tile_hot[k % 2]), over(name[j], COLS), ALU.mult).then_inc(slots_hot, 1)
                dve.wait_ge(slots_named, TOPK * PARTS)
                then(dve.tensor_copy(named[:, :], name_ps[:, 0:COLS]))
                then(dve.tensor_scalar(dest[:, :], named[:, :], 0.0, 2.0 * ROWS_OUT, ALU.is_equal, ALU.mult))
                then(dve.tensor_tensor(dest[:, :], dest[:, :], named[:, :], ALU.add))
                then(dve.tensor_scalar(dest_of[:, :], dest[:, :], -1.0, None, ALU.add))
                then(dve.tensor_scalar(row_i[:, :], named[:, :], -1.0, 0.0, ALU.add, ALU.max))
                then(dve.tensor_scalar(row_of[:, :], row_i[:, :], TOPK.bit_length() - 1, None, ALU.logical_shift_right))


def run_experts(nc, a):
    own = ExitStack()
    with own:
        sb = lambda name, shape, dt=F32: own.enter_context(nc.sbuf_tensor(name, shape, dt))
        sem = lambda name: own.enter_context(nc.semaphore("x_" + name))
        ps = lambda name: own.enter_context(nc.psum_tensor(name, [P, 512], F32))
        ident, expert_of, row_of, dest_of, wup, wdn, bup, bdn = (a[n] for n in ("ident", "expert_of", "row_of", "dest_of", "wup", "wdn", "bup", "bdn"))
        HALF = F // 2
        rows = [sb(f"x_rows{k}", [P, D]) for k in range(2)]; rows_t = sb("x_rows_t", [P, DC, P])
        pre = [sb(f"x_pre{h}", [P, HALF]) for h in range(2)]
        act_t = [sb(f"x_act{h}", [P, HALF]) for h in range(2)]
        y = [sb(f"x_y{k}", [P, D]) for k in range(2)]
        row_now = [sb(f"x_row_now{k}", [P, 1], I32) for k in range(2)]; dest_now = [sb(f"x_dest_now{k}", [P, 1], U32) for k in range(2)]
        rt_ps, y_ps = ps("x_rt_ps"), ps("x_y_ps")
        up_ps = [ps(f"x_up_ps{h}") for h in range(2)]; at_ps = [ps(f"x_at_ps{h}") for h in range(2)]
        turned, rows_ready, up_ready, pre_ready, act_turned, act_ready, y_ready, y_done = (
            sem(n) for n in ("turned", "rows_ready", "up_ready", "pre_ready", "act_turned", "act_ready", "y_ready", "y_done"))
        loaded, y_stored = ([sem(f"{n}{k}") for k in range(2)] for n in ("loaded", "y_stored"))
        y_free, pool_step, pool_passed = sem("y_free"), sem("pool_step"), sem("pool_passed")
        LAST = SLOT_TILES - 1

        with nc.Block() as block:
            @block.sync
            def _(sp):
                sp.sem_inc(turned, 2)
                sp.sem_inc(rows_ready, 1)
                sp.sem_inc(pre_ready, 2)
                sp.sem_inc(act_ready, 2)
                sp.sem_inc(y_done, 1)
                sp.sem_inc(y_free, 2)
                sp.wait_ge(a["w_loaded"], 16 * (3 * E + 2))

        with nc.Block() as block:
            @block.gpsimd
            def _(pool):
                def column(z, n):
                    return z[:, n:n + 1] if isinstance(n, int) else z[:, bass.ds(n, 1)]

                def load(n, k, copies):
                    wait_alone(pool, turned, n + 1, pool_passed)
                    pool.tensor_copy(row_now[k][:, :], column(row_of, n)).then_inc(pool_step, 1)
                    wait_alone(pool, pool_step, copies + 1, pool_passed)
                    pool.indirect_dma_start(rows[k][:, :], None, a["hn_d"].rearrange("b p t n -> (b p t) n"),
                                            bass.IndirectOffsetOnAxis(ap=row_now[k][:, :].bitcast(U32), axis=0)).then_inc(loaded[k], 16)

                def store(n, k, use, copies):
                    wait_alone(pool, y_done, n + 2, pool_passed)
                    pool.tensor_copy(dest_now[k][:, :], column(dest_of, n)).then_inc(pool_step, 1)
                    wait_alone(pool, pool_step, copies + 1, pool_passed)
                    pool.indirect_dma_start(a["y_d"].rearrange("b p t n -> (b p t) n"), bass.IndirectOffsetOnAxis(ap=dest_now[k][:, :], axis=0),
                                            y[k][:, :], None, bounds_check=ROWS_OUT - 1, oob_is_err=False).then_inc(y_stored[k], 16)
                    pool.wait_ge(y_stored[k], use * 16 + 16)
                    pool.sem_inc(y_free, 1)

                for n in range(3):
                    load(n, n % 2, n)
                with pool.Fori(0, LAST // 2) as it:
                    for k in range(2):
                        n = it * 2 + k + 1
                        load(n + 2, 1 - k, it * 4 + k * 2 + 3)
                        store(n - 1, k, it, it * 4 + k * 2 + 4)
                store(LAST, LAST % 2, LAST // 2, LAST // 2 * 4 + 3)
                pool.wait_ge(loaded[0], 16 * (LAST // 2 + 2))

            @block.tensor
            def _(pe):
                def expert(n):
                    at = slice(n, n + 1) if isinstance(n, int) else bass.ds(n, 1)
                    return pe.value_load(expert_of[0:1, at], min_val=0, max_val=E - 1)

                def turn(n, k, use):
                    pe.wait_ge(loaded[k], use * 16 + 16)
                    pe.wait_ge(rows_ready, n + 1)
                    for c in range(DC):
                        last = pe.transpose(rt_ps[:, c * P:(c + 1) * P], rows[k][:, c * P:(c + 1) * P], ident[:, :])
                    last.then_inc(turned, 1)

                def up(n, x):
                    pe.wait_ge(rows_ready, n + 2)
                    for h in range(2):
                        pe.wait_ge(pre_ready, n * 2 + h + 1)
                        for c in range(DC):
                            last = pe.matmul(up_ps[h][:, :], rows_t[:, c, :], wup[:, c, bass.ds(x, 1), h * HALF:(h + 1) * HALF].rearrange("p e f -> p (e f)"),
                                             start=c == 0, stop=c == DC - 1)
                        last.then_inc(up_ready, 1)

                def turn_hidden(n):
                    for h in range(2):
                        pe.wait_ge(pre_ready, n * 2 + h + 3)
                        pe.wait_ge(act_ready, n * 2 + h + 1)
                        for f in range(FC // 2):
                            last = pe.transpose(at_ps[h][:, f * P:(f + 1) * P], pre[h][:, f * P:(f + 1) * P], ident[:, :])
                        last.then_inc(act_turned, 1)

                def down(n, x):
                    pe.wait_ge(y_done, n + 1)
                    pe.wait_ge(act_ready, n * 2 + 4)
                    for f in range(FC):
                        h, g = divmod(f, FC // 2)
                        last = pe.matmul(y_ps[:, 0:D], act_t[h][:, g * P:(g + 1) * P], wdn[:, bass.ds(x, 1), f, :].rearrange("p e n -> p (e n)"),
                                         start=f == 0, stop=f == FC - 1)
                    last.then_inc(y_ready, 1)

                turn(0, 0, 0)
                up(0, expert(0))
                turn(1, 1, 0)
                turn_hidden(0)
                with pe.Fori(0, LAST // 2) as it:
                    for k in range(2):
                        n = it * 2 + k + 1
                        x_last, x = expert(n - 1), expert(n)
                        up(n, x)
                        turn(n + 1, k, it + 1)
                        down(n - 1, x_last)
                        turn_hidden(n)
                down(LAST, expert(LAST))

            @block.scalar
            def _(act):
                def copy_rows(n):
                    act.wait_ge(turned, n + 3)
                    act.activation(rows_t[:, :, :].rearrange("p c t -> p (c t)"), rt_ps[:, 0:DC * P], ACT.Copy).then_inc(rows_ready, 1)

                def gelu(n):
                    for h in range(2):
                        act.wait_ge(act_turned, n * 2 + h + 1)
                        act.activation(act_t[h][:, :], at_ps[h][:, :], ACT.Gelu_apprx_tanh).then_inc(act_ready, 1)

                copy_rows(0)
                copy_rows(1)
                gelu(0)
                with act.Fori(0, LAST // 2) as it:
                    for k in range(2):
                        n = it * 2 + k + 1
                        copy_rows(n + 1)
                        gelu(n)

            @block.vector
            def _(dve):
                def expert(n):
                    at = slice(n, n + 1) if isinstance(n, int) else bass.ds(n, 1)
                    return dve.value_load(expert_of[0:1, at], min_val=0, max_val=E - 1)

                def add_up(n, x):
                    for h in range(2):
                        dve.wait_ge(up_ready, n * 2 + h + 1)
                        dve.tensor_tensor(pre[h][:, :], up_ps[h][:, :], bup[:, bass.ds(x, 1), h * HALF:(h + 1) * HALF].rearrange("p e f -> p (e f)"),
                                          ALU.add).then_inc(pre_ready, 1)

                def add_down(n, k, x):
                    dve.wait_ge(y_free, n + 1)
                    dve.wait_ge(y_ready, n + 1)
                    dve.tensor_tensor(y[k][:, :], y_ps[:, 0:D], bdn[:, bass.ds(x, 1), :].rearrange("p e n -> p (e n)"), ALU.add).then_inc(y_done, 1)

                add_up(0, expert(0))
                with dve.Fori(0, LAST // 2) as it:
                    for k in range(2):
                        n = it * 2 + k + 1
                        x_last, x = expert(n - 1), expert(n)
                        add_up(n, x)
                        add_down(n - 1, k, x_last)
                add_down(LAST, LAST % 2, expert(LAST))


def combine(nc, a):
    own = ExitStack()
    with own:
        sb = lambda name, shape, dt=F32: own.enter_context(nc.sbuf_tensor(name, shape, dt))
        ring = range(RING)
        sems = lambda name: [own.enter_context(nc.semaphore(f"c_{name}{q}")) for q in ring]
        tanh_g, share_of = a["tanh_g"], a["share_of"]
        g2 = sb("c_g2", [P, D]); b2 = sb("c_b2", [P, D])
        hb = [sb(f"c_h{q}", [P, QT, D]) for q in ring]; xb = [sb(f"c_x{q}", [P, QT, D]) for q in ring]
        yb = [sb(f"c_y{q}", [P, QT * TOPK, D]) for q in ring]
        share = [sb(f"c_share{q}", [P, QT, TOPK]) for q in ring]
        stats = sb("c_stats", [P, QT, 6]); mv = sb("c_mv", [P, QT, 2]); rstd = [sb(f"c_rstd{q}", [P, QT]) for q in ring]
        root_v = sb("c_root_v", [P, QT]); root_w = sb("c_root_w", [P, QT])
        shift = [sb(f"c_shift{q}", [P, QT]) for q in ring]
        loaded, moments, normed, x_ready, finished, out_stored = (sems(n) for n in ("loaded", "moments", "normed", "x_ready", "finished", "out_stored"))
        small, rows_ready, step, passed, sp_passed, act_passed = (
            own.enter_context(nc.semaphore(f"c_{n}")) for n in ("small", "rows_ready", "step", "passed", "sp_passed", "act_passed"))

        with nc.Block() as block:
            @block.sync
            def _(sp):
                sp.dma_start(g2[:, :], a["ln2_g"].partition_broadcast(P)).then_inc(small, 16)
                sp.dma_start(b2[:, :], a["ln2_b"].partition_broadcast(P)).then_inc(small, 16)
                for q in ring:
                    sp.sem_inc(out_stored[q], 32)

            @block.vector
            def _(dve):
                dve.wait_ge(small, 32)
                for z in (g2, b2):
                    dve.tensor_scalar(z[:, :], z[:, :], tanh_g[:, 3:4], None, ALU.mult).then_inc(rows_ready, 1)
                dve.wait_ge(rows_ready, 2)

        with nc.Block() as block:
            @block.sync
            def _(sp):
                with sp.Fori(0, PAIRS // RING) as it:
                    for q in ring:
                        free, first = sp.snap(it * 32 + 32), sp.snap(it * 2 * RING + q * 2)
                        wait_alone(sp, out_stored[q], free, sp_passed)
                        sp.dma_start(flat_pair(hb[q]), pair(a["hn_d"], first)).then_inc(loaded[q], 16)
                        sp.dma_start(flat_pair(xb[q]), pair(a["x3_d"], first)).then_inc(loaded[q], 16)
                        sp.dma_start(flat_pair(yb[q]), pair(a["y_d"], first)).then_inc(loaded[q], 16)
                for q in ring:
                    sp.wait_ge(out_stored[q], 32 * (PAIRS // RING + 1))

            @block.gpsimd
            def _(pool):
                with pool.Fori(0, PAIRS // RING) as it:
                    row = lambda z: z[:, :].unsqueeze(1).broadcast_to([P, QT, D])
                    for q in ring:
                        pool.wait_ge(loaded[q], it * 48 + 48)
                        pool.tensor_tensor(xb[q][:, :, :], xb[q][:, :, :], row(b2), ALU.add).then_inc(x_ready[q], 1)
                        pool.wait_ge(x_ready[q], it + 1)
                        pool.sem_inc(passed, 1)

            @block.scalar
            def _(act):
                with act.Fori(0, PAIRS // RING) as it:
                    def store(q):
                        wait_alone(act, finished[q], done, act_passed)
                        for b in range(2):
                            act.dma_start(a["out"][bass.ds(batch[q][b], 1)].rearrange("o (t p) d -> p (o t) d", p=P),
                                          hb[q][:, b * NT:(b + 1) * NT, :]).then_inc(out_stored[q], 16)

                    done, batch = act.snap(it + 1), [[act.snap(it * 2 * RING + q * 2 + b) for b in range(2)] for q in ring]
                    for q in ring:
                        act.wait_ge(moments[q], it + 1)
                        for t in range(QT):
                            last = act.activation(hb[q][:, t, :], hb[q][:, t, :], ACT.Identity, bias=shift[q][:, t:t + 1], scale=rstd[q][:, t:t + 1])
                        last.then_inc(normed[q], 1)
                        if q:
                            store(q - 1)
                    store(RING - 1)

            @block.vector
            def _(dve):
                with dve.Fori(0, PAIRS // RING) as it:
                    s = Steps(dve, step, it, COMBINE_STEPS, passed)
                    row = lambda z: z[:, :].unsqueeze(1).broadcast_to([P, QT, D])
                    for q in ring:
                        s.done(dve.tensor_copy(share[q][:, :, :], share_of[:, bass.ds(it * RING * QT + q * QT, QT), :]))
                    def add_residual(q):
                        dve.wait_ge(normed[q], it + 1)
                        s.done(dve.tensor_tensor(hb[q][:, :, :], hb[q][:, :, :], row(g2), ALU.mult))
                        s.wait()
                        dve.wait_ge(x_ready[q], it + 1)
                        dve.tensor_tensor(hb[q][:, :, :], hb[q][:, :, :], xb[q][:, :, :], ALU.add).then_inc(finished[q], 1)

                    for q in ring:
                        dve.wait_ge(loaded[q], it * 48 + 48)
                        s.wait()
                        for j in range(TOPK):
                            for t in range(QT):
                                s.done(dve.scalar_tensor_tensor(out=hb[q][:, t, :], in0=yb[q][:, t * TOPK + j, :], scalar=share[q][:, t, j:j + 1],
                                                                in1=hb[q][:, t, :], op0=ALU.mult, op1=ALU.add))
                            s.wait()
                        norm_moments(dve, s, hb[q], stats, mv, rstd[q], root_v, root_w, QT)
                        dve.scalar_tensor_tensor(out=shift[q][:, :], in0=mv[:, :, 0], scalar=-1.0, in1=rstd[q][:, :],
                                                 op0=ALU.mult, op1=ALU.mult).then_inc(moments[q], 1)
                        if q:
                            add_residual(q - 1)
                    add_residual(RING - 1)
                    assert s.n == COMBINE_STEPS, s.n


_INS = ['x', 'ctx_2048', 'itok_Bx1_68_817', 'g_xattn', 'g_ffn', 'L0_xattn_b', 'L0_ffn_W_qkv', 'L0_ffn_b_qkv', 'L0_ffn_W_gate',
        'L0_ffn_b_gate', 'L0_ffn_W_experts', 'L0_ffn_b_experts', 'L1_xattn_w_qkv', 'L1_xattn_w_proj', 'L1_xattn_b_proj',
        'L1_ffn_w_qkv', 'L1_ffn_w_o', 'L1_ffn_g1', 'L1_ffn_b1', 'L1_ffn_wg', 'L1_ffn_w1', 'L1_ffn_bb1', 'L1_ffn_w2', 'L1_ffn_bb2',
        'L1_ffn_g2', 'L1_ffn_b2']


def kernel(**inputs):
    import numpy as _np
    import concourse.bacc as _bacc
    from concourse import mybir as _mybir
    from concourse.bass_utils import run_bass_kernel_spmd as _run

    nc = _bacc.Bacc("TRN2", target_bir_lowering=False, num_devices=1)
    arrays, args = {}, []
    for name in _INS:
        arr = _np.ascontiguousarray(inputs[name])
        arrays[f"in_{name}"] = arr
        args.append(nc.dram_tensor(f"in_{name}", arr.shape, _mybir.dt.from_np(arr.dtype), kind="ExternalInput").ap())
    args.append(nc.dram_tensor("out_0", [B, T, D], F32, kind="ExternalOutput").ap())
    build(nc, *args)
    r = _run(nc, [arrays], core_ids=[0])
    return r.results[0]["out_0"]
```
